# Optimizing a Trainium2 kernel written in Bass

```python
import numpy as np
import jax
import jax.numpy as jnp

def _softmax(x, axis=-1):
    return jax.nn.softmax(x, axis=axis)

def _gelu(x):
    return jax.nn.gelu(x, approximate=True)

def _silu(x):
    return jax.nn.silu(x)

def _sigmoid(x):
    return jax.nn.sigmoid(x)

def _layernorm(x, axis=-1, eps=1e-05):
    m = jnp.mean(x, axis=axis, keepdims=True)
    v = jnp.var(x, axis=axis, keepdims=True)
    return (x - m) / jnp.sqrt(v + eps)

def _scatter_add(tgt, idx, src, axis=0):
    return tgt.at[idx].add(src)

def _segment_sum(src, seg, n):
    return jax.ops.segment_sum(src, seg, n)
kernel_name = 'mk_adj_resnorm_d2_adj_r2_eb3365'

def setup_inputs(seed: int=0):
    np.random.seed(seed)
    _w = jnp.asarray

    def _rec_inputs():
        import jax
        import jax.numpy as jnp
        _gk = jax.random.key(seed)
        x = 1.071e-05 + 0.05001 * jax.random.normal(jax.random.fold_in(_gk, 1), (3072, 128), jnp.float32)
        _a = jax.random.bernoulli(jax.random.fold_in(_gk, 2), 0.00520833, (3072, 3072))
        _a = jnp.logical_or(_a, jnp.eye(3072, dtype=bool))
        _af = _a.astype(jnp.float32)
        _af = _af * jax.random.uniform(jax.random.fold_in(_gk, 3), (3072, 3072), jnp.float32, 0.05, 0.00016276)
        adj = _af
        return (x, adj)
    x, adj = _rec_inputs()

    def _L0_gnn_setup():
        import jax, jax.numpy as jnp
        import numpy as np
        N = 3072
        H = 128
        HEADS = 2
        BLOCKS = 2
        TOPK = 3
        key = jax.random.key(seed)
        ks = jax.random.split(key, 10)
        s = 0.05
        hidden = jax.random.normal(ks[0], (N, H), jnp.float32) * s
        A_Global = jax.random.uniform(ks[1], (N, N), jnp.float32) * (1.0 / N)
        w_h = jax.random.normal(ks[2], (3 * H, H), jnp.float32) * s
        w_hf = jax.random.normal(ks[3], (2 * H, H), jnp.float32) * s
        wq = jax.random.normal(ks[4], (BLOCKS, H, H), jnp.float32) * s
        wk = jax.random.normal(ks[5], (BLOCKS, H, H), jnp.float32) * s
        wv = jax.random.normal(ks[6], (BLOCKS, H, H), jnp.float32) * s
        ffn_w = jax.random.normal(ks[7], (BLOCKS, H, H), jnp.float32) * s
        ffn_b = jax.random.normal(ks[8], (BLOCKS, H), jnp.float32) * s
        return {'hidden': hidden, 'A_Global': A_Global, 'w_h': w_h, 'w_hf': w_hf, 'wq': wq, 'wk': wk, 'wv': wv, 'ffn_w': ffn_w, 'ffn_b': ffn_b}
    _L0_gnn_all = _L0_gnn_setup()
    _L0_gnn_in = {k: v for k, v in _L0_gnn_all.items() if k in ('w_h', 'w_hf', 'wq', 'wk', 'wv', 'ffn_w', 'ffn_b')}
    del _L0_gnn_all

    def _L1_gnn_setup():
        import jax, jax.numpy as jnp
        import numpy as np
        N, D_IN, D_HID, D_OUT, K = (5000, 128, 128, 128, 3)

        def cheb_conv(x, L, W, b):
            Tx0 = x
            out = Tx0 @ W[0]
            Tx1 = L @ x
            out = out + Tx1 @ W[1]
            for k in range(2, W.shape[0]):
                Tx2 = 2.0 * (L @ Tx1) - Tx0
                out = out + Tx2 @ W[k]
                Tx0, Tx1 = (Tx1, Tx2)
            return out + b
        key = jax.random.key(seed)
        ks = jax.random.split(key, 4)
        x = jax.random.normal(ks[0], (N, D_IN), dtype=jnp.float32)
        L = jax.random.normal(ks[1], (N, N), dtype=jnp.float32) / jnp.sqrt(jnp.float32(N))
        W0 = jax.random.normal(ks[2], (K, D_IN, D_HID), dtype=jnp.float32) / jnp.sqrt(jnp.float32(D_IN))
        b0 = jnp.zeros((D_HID,), dtype=jnp.float32)
        W1 = jax.random.normal(ks[3], (K, D_HID, D_OUT), dtype=jnp.float32) / jnp.sqrt(jnp.float32(D_HID))
        b1 = jnp.zeros((D_OUT,), dtype=jnp.float32)
        return {'x': x, 'L': L, 'W0': W0, 'b0': b0, 'W1': W1, 'b1': b1}
    _L1_gnn_all = _L1_gnn_setup()
    _L1_gnn_in = {k: v for k, v in _L1_gnn_all.items() if k in ('W0', 'b0', 'W1', 'b1')}
    del _L1_gnn_all
    return {'x': x, 'adj': adj, 'L0_gnn_w_h': _L0_gnn_in['w_h'], 'L0_gnn_w_hf': _L0_gnn_in['w_hf'], 'L0_gnn_wq': _L0_gnn_in['wq'], 'L0_gnn_wk': _L0_gnn_in['wk'], 'L0_gnn_wv': _L0_gnn_in['wv'], 'L0_gnn_ffn_w': _L0_gnn_in['ffn_w'], 'L0_gnn_ffn_b': _L0_gnn_in['ffn_b'], 'L1_gnn_W0': _L1_gnn_in['W0'], 'L1_gnn_b0': _L1_gnn_in['b0'], 'L1_gnn_W1': _L1_gnn_in['W1'], 'L1_gnn_b1': _L1_gnn_in['b1']}

def reference(x, adj, L0_gnn_w_h, L0_gnn_w_hf, L0_gnn_wq, L0_gnn_wk, L0_gnn_wv, L0_gnn_ffn_w, L0_gnn_ffn_b, L1_gnn_W0, L1_gnn_b0, L1_gnn_W1, L1_gnn_b1):
    import jax
    import jax.numpy as jnp

    def _L0_gnn_ref(hidden, A_Global, w_h, w_hf, wq, wk, wv, ffn_w, ffn_b):
        import jax, jax.numpy as jnp
        import numpy as np
        N = 3072
        H = 128
        HEADS = 2
        BLOCKS = 2
        TOPK = 3
        dh = H // HEADS
        corr = hidden @ hidden.T
        corr = corr / jnp.linalg.norm(corr, axis=1, keepdims=True)
        A = A_Global + corr
        hw = hidden @ w_h.T
        h0, h1, h2 = jnp.split(hw, 3, axis=-1)
        f = A @ h0 @ w_hf.T
        f0, f1 = jnp.split(f, 2, axis=-1)
        x = h2 + jax.nn.relu(f0 + h1) * f1

        def split_heads(z):
            return z.reshape(N, HEADS, dh).transpose(1, 0, 2)
        for b in range(BLOCKS):
            q = split_heads(x @ wq[b].T)
            k = split_heads(x @ wk[b].T)
            v = split_heads(x @ wv[b].T)
            score = jnp.tanh(jnp.einsum('hnd,hmd->hnm', q, k))
            att = jnp.einsum('hnm,hmd->hnd', score, v)
            att = att.transpose(1, 0, 2).reshape(N, H)
            x = x + jax.nn.relu(att @ ffn_w[b].T + ffn_b[b])
        fenzi = x @ x.T
        fl = jnp.sqrt(jnp.sum(x * x + 1e-06, axis=1, keepdims=True))
        cos_sim = jax.nn.softmax(fenzi / (fl @ fl.T), axis=-1)
        top_v, top_i = jax.lax.top_k(cos_sim, TOPK)
        cw = jax.nn.softmax(top_v, axis=-1)
        neighbor_sess = jnp.sum(cw[..., None] * x[top_i], axis=1)
        return neighbor_sess

    def _L1_gnn_ref(x, L, W0, b0, W1, b1):
        import jax, jax.numpy as jnp
        import numpy as np
        N, D_IN, D_HID, D_OUT, K = (5000, 128, 128, 128, 3)

        def cheb_conv(x, L, W, b):
            Tx0 = x
            out = Tx0 @ W[0]
            Tx1 = L @ x
            out = out + Tx1 @ W[1]
            for k in range(2, W.shape[0]):
                Tx2 = 2.0 * (L @ Tx1) - Tx0
                out = out + Tx2 @ W[k]
                Tx0, Tx1 = (Tx1, Tx2)
            return out + b
        h = jax.nn.elu(cheb_conv(x, L, W0, b0))
        h = jax.nn.elu(cheb_conv(h, L, W1, b1))
        return h
    x = _layernorm(x + _L0_gnn_ref(x, adj, L0_gnn_w_h, L0_gnn_w_hf, L0_gnn_wq, L0_gnn_wk, L0_gnn_wv, L0_gnn_ffn_w, L0_gnn_ffn_b), axis=-1)
    x = _layernorm(x + _L1_gnn_ref(x, adj, L1_gnn_W0, L1_gnn_b0, L1_gnn_W1, L1_gnn_b1), axis=-1)
    return x

_drawn_inputs = setup_inputs


def setup_inputs(seed=0):
    import zlib

    import numpy as np

    out = dict(_drawn_inputs(seed))
    spreads = {'L1_gnn_b0': (0.0, 0.1), 'L1_gnn_b1': (0.0, 0.1)}
    factors = {}
    for name, (base, spread) in spreads.items():
        noise = np.random.default_rng([zlib.crc32(name.encode()), seed]).standard_normal(out[name].shape)
        drawn = base * np.exp(spread * noise) if base else spread * noise
        out[name] = jnp.asarray(drawn.astype(out[name].dtype))
    for name, factor in factors.items():
        out[name] = (out[name] * factor).astype(out[name].dtype)
    return out
```

```python
from contextlib import ExitStack

import concourse.bass as bass
from concourse import mybir

P = 128
F32 = mybir.dt.float32
F32R = mybir.dt.float32r
U32 = mybir.dt.uint32
ALU = mybir.AluOpType
ACT = mybir.ActivationFunctionType
AX_X = mybir.AxisListType.X

N = 3072
TW = 512
TILES = N // TW
BLOCKS = N // P
BPT = TW // P
CH = 4
CHUNKS = BLOCKS // CH
HEADS = 2
DH = P // HEADS
LAYERS = 2
SLOTS = 3
TOP = 3
CREDIT = 1


def tile(t, base=0):
    return bass.ds(t * TW + base, TW)


def gnn_kernel(nc, x_rows, x_cols, adj_t, w_h, w_hf, wq, wk, wv, ffn_w, ffn_b, cheb_w, cheb_b, out):
    with ExitStack() as ctx:
        def sb(name, width, dt=F32):
            return ctx.enter_context(nc.sbuf_tensor(name, [P, width], dt))

        def sem(name):
            return ctx.enter_context(nc.semaphore(name))

        def sems(name, n):
            return [sem(f"{name}{i}") for i in range(n)]

        ps = ctx.enter_context(nc.psum_tensor("ps", [P, 8 * TW], F32))

        def bank(k):
            return ps[:, k * TW:(k + 1) * TW]

        plane_x = sb("plane_x", N)
        plane_y = sb("plane_y", N)
        plane_v = sb("plane_v", N)
        pair = sb("pair", 2 * N)
        ring = sb("ring", CHUNKS * CH * TW)
        with ExitStack() as early:
            def split(name):
                return early.enter_context(nc.sbuf_tensor(name, [P, N], F32R))

            k_split = [split(f"k_split{h}") for h in range(HEADS)]
            q_hi = [split(f"q_hi{h}") for h in range(HEADS)]
            q_lo = [split(f"q_lo{h}") for h in range(HEADS)]
        plane_h = sb("plane_h", N)
        spare = sb("spare", 5 * N)

        wh_s = sb("wh_s", 3 * P)
        whf_s = sb("whf_s", 2 * P)
        wq_s = sb("wq_s", LAYERS * HEADS * P)
        wk_s = sb("wk_s", LAYERS * HEADS * P)
        wv_s = sb("wv_s", LAYERS * P)
        ffn_s = sb("ffn_s", LAYERS * P)
        ffnb_s = sb("ffnb_s", LAYERS)
        cheb_s = sb("cheb_s", LAYERS * 3 * P)
        chebb_s = sb("chebb_s", LAYERS)
        ident = sb("ident", P)
        ones = sb("ones", P)
        gram = sb("gram", 2 * P)
        stage = sb("stage", TW)
        tmp_a = sb("tmp_a", TW)
        tmp_b = sb("tmp_b", TW)
        tmp_c = sb("tmp_c", TW)
        block_split = [sb(f"block_split{i}", 2 * P, F32R) for i in range(2)]
        top_v = sb("top_v", BLOCKS * 8)
        top_i = sb("top_i", BLOCKS * 8, U32)
        small = sb("small", 8 * TOP * BLOCKS)

        y_dram = nc.dram_tensor("y_scratch", [N, P], F32)

        x_t = plane_x
        xh = pair[:, :].rearrange("p (j c) -> p j c", c=2 * P)
        y_t = plane_y
        probs = [ring[:, s * 2 * TW:(s + 1) * 2 * TW] for s in range(SLOTS)]

        loaded = sem("loaded")
        ones_set = sem("ones_set")
        ident_set = sem("ident_set")
        adj_in = sems("adj_in", CHUNKS)
        chunk_used = sem("chunk_used")

        def adj_pass(pe, n_pass, t, rows, before_last=None):
            for c in range(CHUNKS):
                pe.wait_ge(adj_in[c], 16 * (TILES * n_pass + 1) + 16 * t)
                for b in range(CH):
                    j = c * CH + b
                    mm = pe.matmul(ps[:, tile(t)], rows(j), ring[:, (c * CH + b) * TW:(c * CH + b + 1) * TW],
                                   start=(j == 0), stop=(j == BLOCKS - 1))
                mm.then_inc(chunk_used, 1)

        h0_ready, h0_kept = sem("h0_ready"), sem("h0_kept")
        gram_ready, gram_kept = sem("gram_ready"), sem("gram_kept")
        gx_ready, gx_kept = sem("gx_ready"), sem("gx_kept")
        norm_ready, corr_ready = sem("norm_ready"), sem("corr_ready")
        root_ready, front_step = sem("root_ready"), sem("front_step")
        gate_ready, gate_kept, y_kept = sem("gate_ready"), sem("gate_kept"), sem("y_kept")
        agg_kept = sem("agg_kept")
        staged = sems("staged", LAYERS)
        proj = sems("proj", LAYERS)
        proj_hi = sems("proj_hi", LAYERS)
        proj_lo = sems("proj_lo", LAYERS)
        scores = sems("scores", LAYERS)
        tanhs = sems("tanhs", LAYERS)
        probs_used = sems("probs_used", LAYERS)
        att_kept = sems("att_kept", LAYERS)
        ffn_ready = sems("ffn_ready", LAYERS)
        relu_kept = sems("relu_kept", LAYERS)
        y_new = sems("y_new", LAYERS)
        sq_kept, sum_ready = sem("sq_kept"), sem("sum_ready")
        y_turned, y_rows_kept, y_out = sem("y_turned"), sem("y_rows_kept"), sem("y_out")
        unit_step, unit_root, unit_hi, unit_lo = sem("unit_step"), sem("unit_root"), sem("unit_hi"), sem("unit_lo")
        y_staged = sem("y_staged")
        block_staged, cos_ready, cos_kept = sem("block_staged"), sem("cos_ready"), sem("cos_kept")
        exp_done, top_done, index_done = sem("exp_done"), sem("top_done"), sem("index_done")
        gathered = sems("gathered", BLOCKS)
        x_again = sem("x_again")
        weight_step, weight_act = sem("weight_step"), sem("weight_act")
        mix_step, mix_act, x1_ready, x1_turned, x1_cols = (
            sem("mix_step"), sem("mix_act"), sem("x1_ready"), sem("x1_turned"), sem("x1_cols"))
        a_kept = sems("a_kept", LAYERS)
        a_turned = sems("a_turned", LAYERS)
        a_rows = sems("a_rows", LAYERS)
        t2_kept = sems("t2_kept", LAYERS)
        mix_ready = sems("mix_ready", LAYERS)
        pos_kept = sems("pos_kept", LAYERS)
        neg_kept = sems("neg_kept", LAYERS)
        exp_kept = sems("exp_kept", LAYERS)
        h_kept = sems("h_kept", LAYERS)
        h_turned = sems("h_turned", LAYERS)
        h_rows = sems("h_rows", LAYERS)
        ln_step, ln_act, root_kept = sem("ln_step"), sem("ln_act"), sem("root_kept")
        row_out, stored = sem("row_out"), sem("stored")

        credited = [y_kept, sum_ready, y_turned, y_rows_kept, unit_hi, unit_lo, row_out, stored,
                    *y_new, *proj_lo, *proj, *att_kept, *relu_kept, *ffn_ready, *a_rows, *h_kept, *h_rows,
                    *mix_ready]

        block = ctx.enter_context(nc.Block())

        cos_rows = [pair[:, i * N:(i + 1) * N] for i in range(2)]
        unit_hi_t, unit_lo_t = q_hi[0], q_lo[0]
        gather_v = ring[:, 0:BLOCKS * TOP * P].rearrange("p (j k d) -> p j k d", k=TOP, d=P)
        n_small = TOP * BLOCKS

        def sm(i, w=n_small):
            return small[:, i * n_small:i * n_small + w]

        z_rows = [plane_x, plane_h]
        z_cols = [plane_y[:, :], pair[:, N:2 * N]]
        a_rows_v = plane_v
        a_cols = pair[:, 0:N]

        def w_cheb(layer, k):
            return cheb_s[:, (layer * 3 + k) * P:(layer * 3 + k + 1) * P]

        @block.sync
        def _(sp):
            def chunk(t, c):
                return sp.dma_start(ring[:, c * CH * TW:(c + 1) * CH * TW],
                                    adj_t[:, bass.ds(t * (BLOCKS * TW) + c * CH * TW, CH * TW)])

            for n_pass in range(1 + 2 * LAYERS):
                first = 0
                if n_pass <= 1:
                    if n_pass == 1:
                        sp.wait_ge(x1_ready, 1)
                    for c in range(CHUNKS):
                        chunk(0, c).then_inc(adj_in[c], 16)
                    first = 1
                with sp.Fori(first, TILES) as t:
                    for c in range(CHUNKS):
                        sp.wait_ge(chunk_used, CHUNKS * (TILES * n_pass - 1) + c + 1 + t * CHUNKS)
                        chunk(t, c).then_inc(adj_in[c], 16)

        @block.gpsimd
        def _(pool):
            for s in credited:
                pool.sem_inc(s, CREDIT)
            pool.memset(ones[:, :], 1.0).then_inc(ones_set, 1)
            pool.memset(ident[:, :], 0.0).then_inc(ident_set, 1)
            pool.wait_ge(ident_set, 1)
            pool.affine_select(out=ident[:, :], in_=ident[:, :], compare_op=ALU.not_equal, fill=1.0, base=0,
                               pattern=[[-1, P]], channel_multiplier=1).then_inc(ident_set, 1)

            pool.wait_ge(y_rows_kept, CREDIT + TILES)
            pool.dma_start(y_dram[:, :].rearrange("(j p) d -> p j d", p=P),
                           plane_v[:, :].rearrange("p (j d) -> p j d", d=P)).then_inc(y_out, 16)
            pool.wait_ge(unit_lo, CREDIT + TILES)
            pool.wait_ge(y_out, 16)
            for j in range(BLOCKS + 1):
                if j < BLOCKS:
                    if j >= 2:
                        pool.wait_ge(cos_ready, TILES * (j - 1))
                    dst = block_split[j % 2]
                    pool.tensor_copy(dst[:, 0:P], unit_hi_t[:, j * P:(j + 1) * P].bitcast(F32))
                    pool.tensor_copy(dst[:, P:2 * P], unit_lo_t[:, j * P:(j + 1) * P].bitcast(F32)).then_inc(
                        block_staged, 1)
                if j >= 1:
                    pool.wait_ge(index_done, j)
                    for k in range(TOP):
                        pool.indirect_dma_start(
                            gather_v[:, j - 1, k, :], None, y_dram[:, :],
                            bass.IndirectOffsetOnAxis(ap=top_i[:, (j - 1) * 8 + k:(j - 1) * 8 + k + 1], axis=0),
                        ).then_inc(gathered[j - 1], 16)

        @block.scalar
        def _(act):
            for dst, src in ((x_t, x_cols), (wh_s, w_h), (whf_s, w_hf), (wq_s, wq), (wk_s, wk), (wv_s, wv),
                             (ffn_s, ffn_w), (ffnb_s, ffn_b), (cheb_s, cheb_w), (chebb_s, cheb_b)):
                act.dma_start(dst[:, :], src).then_inc(loaded, 16)
            act.dma_start(xh[:, :, 0:P], x_rows.rearrange("p (j d) -> p j d", d=P)).then_inc(loaded, 16)

            act.wait_ge(gram_ready, 1)
            act.activation(gram[:, :], bank(6)[:, 0:2 * P], ACT.Copy).then_inc(gram_kept, 1)
            with act.Fori(0, TILES) as t:
                act.wait_ge(norm_ready, t + 1)
                act.wait_ge(y_kept, CREDIT + t)
                act.activation(tmp_b[:, :], bank(7), ACT.Sqrt).then_inc(root_ready, 1)
                act.wait_ge(gate_ready, 2 * t + 1)
                act.activation(tmp_b[:, :], bank(6), ACT.Relu).then_inc(gate_kept, 1)

            for b in range(LAYERS):
                with act.Fori(0, TILES) as t:
                    for k in range(2 * HEADS):
                        act.wait_ge(proj[b], CREDIT + 5 * t + k + 1)
                        dst = (q_hi + k_split)[k]
                        act.activation(dst[:, tile(t)], bank(k), ACT.Copy).then_inc(proj_hi[b], 1)
                act.sem_inc(tanhs[b], SLOTS)
                with act.Fori(0, TILES) as t:
                    for g in range(BLOCKS):
                        s = g % SLOTS
                        act.wait_ge(scores[b], BLOCKS * t + g + 1)
                        act.wait_ge(probs_used[b], BLOCKS * t + g + 1)
                        act.activation(probs[s], ps[:, 2 * s * TW:2 * (s + 1) * TW], ACT.Tanh).then_inc(tanhs[b], 1)
                    act.wait_ge(ffn_ready[b], CREDIT + t + 1)
                    act.wait_ge(y_new[b], CREDIT + t)
                    act.activation(tmp_b[:, :], bank(7), ACT.Relu, bias=ffnb_s[:, b:b + 1]).then_inc(relu_kept[b], 1)

            act.dma_start(plane_x[:, :], x_rows).then_inc(x_again, 16)
            with act.Fori(0, TILES) as t:
                act.wait_ge(unit_step, 6 * t + 1)
                act.activation(tmp_b[:, :], tmp_c[:, :], ACT.Sqrt).then_inc(unit_root, 1)
                act.wait_ge(unit_step, 6 * t + 6)
                act.activation(unit_hi_t[:, tile(t)], tmp_c[:, :], ACT.Copy).then_inc(unit_hi, 1)
            act.wait_ge(unit_lo, CREDIT + TILES)
            for j in range(BLOCKS):
                if j >= 2:
                    act.wait_ge(index_done, j - 1)
                    act.wait_ge(exp_done, j - 1)
                for n in range(TILES):
                    act.wait_ge(cos_ready, TILES * j + n + 1)
                    act.activation(cos_rows[j % 2][:, n * TW:(n + 1) * TW], bank(n), ACT.Copy).then_inc(cos_kept, 1)
                act.wait_ge(cos_kept, TILES * (j + 1))
                if j >= 1:
                    act.wait_ge(exp_done, j)
                act.activation(ring[:, 3 * N:4 * N], cos_rows[j % 2], ACT.Exp, accum_out=sm(0)[:, j:j + 1]).then_inc(
                    exp_done, 1)
            act.wait_ge(index_done, BLOCKS)
            act.activation(sm(1).rearrange("p (j k) -> p j k", k=TOP),
                           top_v[:, :].rearrange("p (j k) -> p j k", k=8)[:, :, 0:TOP], ACT.Exp).then_inc(weight_act, 1)
            act.wait_ge(weight_step, 3)
            act.activation(sm(1), sm(2), ACT.Exp).then_inc(weight_act, 1)
            act.wait_ge(mix_step, 9)
            act.activation(pair[:, 0:N], plane_x[:, :], ACT.Square).then_inc(mix_act, 1)
            act.wait_ge(mix_step, 11)
            act.activation(sm(5)[:, 0:BLOCKS], sm(4)[:, 0:BLOCKS], ACT.Sqrt).then_inc(mix_act, 1)

            for b in range(LAYERS):
                with act.Fori(0, TILES) as t:
                    act.wait_ge(chunk_used, CHUNKS * (TILES * (1 + 2 * b) + 1) + t * CHUNKS)
                    act.wait_ge(a_rows[b], CREDIT + 2 * t)
                    act.activation(stage[:, :], ps[:, tile(t)], ACT.Copy).then_inc(a_kept[b], 1)
                with act.Fori(0, TILES) as t:
                    act.wait_ge(mix_ready[b], CREDIT + t + 1)
                    act.wait_ge(h_kept[b], CREDIT + t)
                    act.activation(tmp_a[:, :], bank(7), ACT.Relu, bias=chebb_s[:, b:b + 1]).then_inc(pos_kept[b], 1)
                    act.wait_ge(neg_kept[b], t + 1)
                    act.activation(tmp_b[:, :], tmp_b[:, :], ACT.Exp).then_inc(exp_kept[b], 1)
                    if b == LAYERS - 1:
                        act.wait_ge(ln_step, 8 * t + 3)
                        act.activation(tmp_c[:, :], stage[:, :], ACT.Square).then_inc(ln_act, 1)
                        act.wait_ge(ln_step, 8 * t + 5)
                        act.activation(sm(5)[:, 0:BPT], sm(4)[:, 0:BPT], ACT.Sqrt).then_inc(ln_act, 1)
                        act.wait_ge(row_out, CREDIT + t + 1)
                        act.dma_start(out[:, bass.ds(t * TW, TW)], tmp_c[:, :]).then_inc(stored, 16)
            act.wait_ge(stored, CREDIT + 16 * TILES)

        @block.tensor
        def _(pe):
            pe.wait_ge(loaded, 16 * 11)
            for j in range(BLOCKS):
                mm = pe.matmul(ps[:, j * P:(j + 1) * P], x_t[:, j * P:(j + 1) * P], wh_s[:, 0:P], start=True, stop=True)
                if j % BPT == BPT - 1:
                    mm.then_inc(h0_ready, 1)
            for j in range(BLOCKS):
                if j % BPT == 0:
                    pe.wait_ge(h0_kept, j // BPT + 1)
                mm = pe.matmul(bank(6)[:, 0:2 * P], xh[:, j, 0:P], xh[:, j, :], start=(j == 0), stop=(j == BLOCKS - 1))
            mm.then_inc(gram_ready, 1)
            pe.wait_ge(gram_kept, 1)
            pe.wait_ge(ones_set, 1)
            with pe.Fori(0, TILES) as t:
                pe.wait_ge(y_kept, CREDIT + t)
                pe.matmul(bank(6), gram[:, 0:P], x_t[:, tile(t)], start=True, stop=True).then_inc(gx_ready, 1)
                pe.wait_ge(gx_kept, t + 1)
                pe.matmul(bank(7), ones[:, :], tmp_a[:, :], start=True, stop=True).then_inc(norm_ready, 1)
                pe.matmul(bank(6), gram[:, P:2 * P], x_t[:, tile(t)], start=True, stop=True).then_inc(corr_ready, 1)
                adj_pass(pe, 0, t, lambda j: xh[:, j, P:2 * P])
                pe.wait_ge(agg_kept, t + 1)
                pe.matmul(bank(6), wh_s[:, P:2 * P], x_t[:, tile(t)], start=True, stop=False)
                pe.matmul(bank(6), whf_s[:, 0:P], stage[:, :], start=False, stop=True).then_inc(gate_ready, 1)
                pe.matmul(bank(7), whf_s[:, P:2 * P], stage[:, :], start=True, stop=True)
                pe.matmul(ps[:, tile(t)], wh_s[:, 2 * P:3 * P], x_t[:, tile(t)], start=True, stop=True).then_inc(
                    gate_ready, 1)

            for b in range(LAYERS):
                with pe.Fori(0, TILES) as t:
                    pe.wait_ge(staged[b], t + 1)
                    pe.wait_ge(proj_lo[b], CREDIT + 5 * t)
                    for k, w in enumerate((wq_s, wq_s, wk_s, wk_s)):
                        h = k % HEADS
                        pe.matmul(bank(k), w[:, (b * HEADS + h) * P:(b * HEADS + h + 1) * P], stage[:, :],
                                  start=True, stop=True).then_inc(proj[b], 1)
                    for q in range(BPT):
                        mm = pe.matmul(bank(4)[:, q * P:(q + 1) * P], stage[:, q * P:(q + 1) * P],
                                       wv_s[:, b * P:(b + 1) * P], start=True, stop=True)
                    mm.then_inc(proj[b], 1)
                pe.wait_ge(proj_lo[b], CREDIT + 5 * TILES)
                pe.sem_inc(probs_used[b], SLOTS)
                with pe.Fori(0, TILES) as t:
                    def score(g):
                        pe.wait_ge(tanhs[b], BLOCKS * t + g + 1)
                        for h in range(HEADS):
                            dst = bank(2 * (g % SLOTS) + h)
                            kb = k_split[h][:, g * P:(g + 1) * P]
                            pe.matmul(dst, kb, q_hi[h][:, tile(t)], start=True, stop=False)
                            mm = pe.matmul(dst, kb, q_lo[h][:, tile(t)], start=False, stop=True)
                        mm.then_inc(scores[b], 1)

                    score(0)
                    score(1)
                    for g in range(BLOCKS):
                        if g + 2 < BLOCKS:
                            score(g + 2)
                        if g == 0:
                            pe.wait_ge(att_kept[b], CREDIT + t)
                        pe.wait_ge(tanhs[b], BLOCKS * t + g + 1 + SLOTS)
                        for h in range(HEADS):
                            mm = pe.matmul(bank(6)[h * DH:(h + 1) * DH, :],
                                           plane_v[:, g * P + h * DH:g * P + (h + 1) * DH],
                                           probs[g % SLOTS][:, h * TW:(h + 1) * TW],
                                           start=(g == 0), stop=(g == BLOCKS - 1))
                        mm.then_inc(probs_used[b], 1)
                    pe.wait_ge(att_kept[b], CREDIT + t + 1)
                    pe.wait_ge(relu_kept[b], CREDIT + t)
                    pe.matmul(bank(7), ffn_s[:, b * P:(b + 1) * P], stage[:, :], start=True, stop=True).then_inc(
                        ffn_ready[b], 1)

            pe.wait_ge(ident_set, 2)
            with pe.Fori(0, TILES) as t:
                pe.wait_ge(sq_kept, t + 1)
                pe.wait_ge(y_rows_kept, CREDIT + t)
                pe.matmul(bank(6), ones[:, :], tmp_a[:, :], start=True, stop=True).then_inc(sum_ready, 1)
                pe.wait_ge(y_staged, t + 1)
                for q in range(BPT):
                    mm = pe.transpose(bank(7)[:, q * P:(q + 1) * P], stage[:, q * P:(q + 1) * P], ident[:, :])
                mm.then_inc(y_turned, 1)
            for j in range(BLOCKS):
                pe.wait_ge(block_staged, j + 1)
                hi, lo = block_split[j % 2][:, 0:P], block_split[j % 2][:, P:2 * P]
                for n in range(TILES):
                    if j >= 1:
                        pe.wait_ge(cos_kept, TILES * (j - 1) + n + 1)
                    cols = slice(n * TW, (n + 1) * TW)
                    pe.matmul(bank(n), hi, unit_hi_t[:, cols], start=True, stop=False)
                    pe.matmul(bank(n), hi, unit_lo_t[:, cols], start=False, stop=False)
                    pe.matmul(bank(n), lo, unit_hi_t[:, cols], start=False, stop=True).then_inc(cos_ready, 1)
            pe.wait_ge(x1_ready, 1)
            for j in range(BLOCKS):
                mm = pe.transpose(ps[:, j * P:(j + 1) * P], plane_x[:, j * P:(j + 1) * P], ident[:, :])
                if j % BPT == BPT - 1:
                    mm.then_inc(x1_turned, 1)
            pe.wait_ge(x1_cols, TILES)

            for b in range(LAYERS):
                zr = z_rows[b]
                with pe.Fori(0, TILES) as t:
                    adj_pass(pe, 1 + 2 * b, t, lambda j: zr[:, j * P:(j + 1) * P])
                    pe.wait_ge(a_kept[b], t + 1)
                    pe.wait_ge(a_rows[b], CREDIT + 2 * t)
                    for q in range(BPT):
                        mm = pe.transpose(bank(6)[:, q * P:(q + 1) * P], stage[:, q * P:(q + 1) * P], ident[:, :])
                    mm.then_inc(a_turned[b], 1)
                pe.wait_ge(a_rows[b], CREDIT + 2 * TILES)
                with pe.Fori(0, TILES) as t:
                    adj_pass(pe, 2 + 2 * b, t, lambda j: a_rows_v[:, j * P:(j + 1) * P])
                    pe.wait_ge(h_kept[b], CREDIT + t)
                    pe.matmul(bank(7), w_cheb(b, 0), z_cols[b][:, tile(t)], start=True, stop=False)
                    pe.matmul(bank(7), w_cheb(b, 1), a_cols[:, tile(t)], start=False, stop=False)
                    pe.wait_ge(t2_kept[b], t + 1)
                    pe.matmul(bank(7), w_cheb(b, 2), stage[:, :], start=False, stop=True).then_inc(mix_ready[b], 1)
                    pe.wait_ge(h_kept[b], CREDIT + t + 1)
                    pe.wait_ge(h_rows[b], CREDIT + t)
                    for q in range(BPT):
                        mm = pe.transpose(bank(6)[:, q * P:(q + 1) * P], tmp_a[:, q * P:(q + 1) * P], ident[:, :])
                    mm.then_inc(h_turned[b], 1)
                if b == 0:
                    pe.wait_ge(h_rows[b], CREDIT + TILES)

        @block.vector
        def _(dve):
            for g in range(TILES):
                dve.wait_ge(h0_ready, g + 1)
                dve.tensor_copy(xh[:, g * BPT:(g + 1) * BPT, P:2 * P],
                                bank(g).rearrange("p (j d) -> p j d", d=P)).then_inc(h0_kept, 1)

            with dve.Fori(0, TILES) as t:
                dve.wait_ge(gx_ready, t + 1)
                dve.tensor_tensor(out=tmp_a[:, :], in0=bank(6), in1=x_t[:, tile(t)], op=ALU.mult).then_inc(gx_kept, 1)
                dve.wait_ge(root_ready, t + 1)
                dve.reciprocal(tmp_c[:, :], tmp_b[:, :]).then_inc(front_step, 1)
                dve.wait_ge(front_step, 6 * t + 1)
                dve.tensor_tensor(out=tmp_c[:, :], in0=bank(7), in1=tmp_c[:, :], op=ALU.mult).then_inc(front_step, 1)
                dve.wait_ge(front_step, 6 * t + 2)
                dve.tensor_tensor(out=tmp_c[:, :], in0=tmp_b[:, :], in1=tmp_c[:, :], op=ALU.add).then_inc(front_step, 1)
                dve.wait_ge(front_step, 6 * t + 3)
                dve.reciprocal(tmp_c[:, :], tmp_c[:, :]).then_inc(front_step, 1)
                dve.wait_ge(front_step, 6 * t + 4)
                dve.wait_ge(corr_ready, t + 1)
                dve.scalar_tensor_tensor(out=tmp_c[:, :], in0=bank(6), scalar=2.0, in1=tmp_c[:, :], op0=ALU.mult,
                                         op1=ALU.mult).then_inc(front_step, 1)
                dve.wait_ge(front_step, 6 * t + 5)
                dve.wait_ge(chunk_used, CHUNKS * t + CHUNKS)
                dve.tensor_tensor(out=stage[:, :], in0=ps[:, tile(t)], in1=tmp_c[:, :], op=ALU.add).then_inc(
                    agg_kept, 1)
                dve.wait_ge(gate_kept, t + 1)
                dve.wait_ge(gate_ready, 2 * t + 2)
                dve.tensor_tensor(out=tmp_b[:, :], in0=bank(7), in1=tmp_b[:, :], op=ALU.mult).then_inc(front_step, 1)
                dve.wait_ge(front_step, 6 * t + 6)
                dve.tensor_tensor(out=y_t[:, tile(t)], in0=ps[:, tile(t)], in1=tmp_b[:, :], op=ALU.add).then_inc(
                    y_kept, 1)
            dve.wait_ge(y_kept, CREDIT + TILES)

            for b in range(LAYERS):
                if b:
                    dve.wait_ge(y_new[b - 1], CREDIT + TILES)
                with dve.Fori(0, TILES) as t:
                    dve.wait_ge(proj[b], CREDIT + 5 * t)
                    dve.tensor_scalar(stage[:, :], y_t[:, tile(t)], 1.0, None, ALU.mult).then_inc(staged[b], 1)
                    for k in range(HEADS):
                        dve.wait_ge(proj_hi[b], 4 * t + k + 1)
                        dve.tensor_tensor(out=q_lo[k][:, tile(t)], in0=bank(k), in1=q_hi[k][:, tile(t)].bitcast(F32),
                                          op=ALU.subtract).then_inc(proj_lo[b], 1)
                    for h in range(HEADS):
                        dve.wait_ge(proj_hi[b], 4 * t + HEADS + h + 1)
                        dst = k_split[h][DH:P, tile(t)]
                        dve.tensor_tensor(out=dst, in0=bank(HEADS + h)[DH:P, :], in1=dst.bitcast(F32),
                                          op=ALU.subtract).then_inc(proj_lo[b], 1)
                    dve.wait_ge(proj[b], CREDIT + 5 * t + 5)
                    dve.tensor_scalar(plane_v[:, tile(t)], bank(4), 1.0, None, ALU.mult).then_inc(proj_lo[b], 1)
                with dve.Fori(0, TILES) as t:
                    dve.wait_ge(probs_used[b], BLOCKS * t + BLOCKS + SLOTS)
                    dve.wait_ge(ffn_ready[b], CREDIT + t)
                    dve.tensor_scalar(stage[:, :], bank(6), 1.0, None, ALU.mult).then_inc(att_kept[b], 1)
                    dve.wait_ge(relu_kept[b], CREDIT + t + 1)
                    dve.tensor_tensor(out=y_t[:, tile(t)], in0=y_t[:, tile(t)], in1=tmp_b[:, :], op=ALU.add).then_inc(
                        y_new[b], 1)
            dve.wait_ge(y_new[LAYERS - 1], CREDIT + TILES)

            with dve.Fori(0, TILES) as t:
                dve.wait_ge(sum_ready, CREDIT + t)
                dve.tensor_tensor(out=tmp_a[:, :], in0=y_t[:, tile(t)], in1=y_t[:, tile(t)], op=ALU.mult).then_inc(
                    sq_kept, 1)
                dve.wait_ge(y_turned, CREDIT + t)
                dve.tensor_scalar(stage[:, :], y_t[:, tile(t)], 1.0, None, ALU.mult).then_inc(y_staged, 1)
                dve.wait_ge(sum_ready, CREDIT + t + 1)
                dve.wait_ge(unit_hi, CREDIT + t)
                dve.wait_ge(unit_lo, CREDIT + t)
                dve.tensor_scalar(tmp_c[:, :], bank(6), P * 1e-6, None, ALU.add).then_inc(unit_step, 1)
                dve.wait_ge(unit_root, t + 1)
                dve.reciprocal(tmp_a[:, :], tmp_b[:, :]).then_inc(unit_step, 1)
                dve.wait_ge(unit_step, 6 * t + 2)
                dve.tensor_tensor(out=tmp_a[:, :], in0=tmp_c[:, :], in1=tmp_a[:, :], op=ALU.mult).then_inc(unit_step, 1)
                dve.wait_ge(unit_step, 6 * t + 3)
                dve.tensor_tensor(out=tmp_a[:, :], in0=tmp_b[:, :], in1=tmp_a[:, :], op=ALU.add).then_inc(unit_step, 1)
                dve.wait_ge(unit_step, 6 * t + 4)
                dve.reciprocal(tmp_a[:, :], tmp_a[:, :]).then_inc(unit_step, 1)
                dve.wait_ge(unit_step, 6 * t + 5)
                dve.scalar_tensor_tensor(out=tmp_c[:, :], in0=y_t[:, tile(t)], scalar=2.0, in1=tmp_a[:, :],
                                         op0=ALU.mult, op1=ALU.mult).then_inc(unit_step, 1)
                dve.wait_ge(unit_hi, CREDIT + t + 1)
                dve.tensor_tensor(out=unit_lo_t[:, tile(t)], in0=tmp_c[:, :], in1=unit_hi_t[:, tile(t)].bitcast(F32),
                                  op=ALU.subtract).then_inc(unit_lo, 1)
                dve.wait_ge(y_turned, CREDIT + t + 1)
                dve.tensor_scalar(plane_v[:, tile(t)], bank(7), 1.0, None, ALU.mult).then_inc(y_rows_kept, 1)

            for j in range(BLOCKS):
                dve.wait_ge(cos_kept, TILES * (j + 1))
                top = top_v[:, j * 8:(j + 1) * 8]
                dve.max(top, cos_rows[j % 2]).then_inc(top_done, 1)
                dve.wait_ge(top_done, j + 1)
                dve.max_index(top_i[:, j * 8:(j + 1) * 8], top, cos_rows[j % 2]).then_inc(index_done, 1)

            def per_block(ap, n=TOP):
                return ap[:, 0:BLOCKS].unsqueeze(2).to_broadcast([P, BLOCKS, n])

            def by_block(ap, k=TOP):
                return ap.rearrange("p (j k) -> p j k", k=k)

            steps = [0]

            def step(ins):
                steps[0] += 1
                ins.then_inc(weight_step, 1)
                dve.wait_ge(weight_step, steps[0])

            dve.wait_ge(exp_done, BLOCKS)
            step(dve.reciprocal(sm(2)[:, 0:BLOCKS], sm(0)[:, 0:BLOCKS]))
            dve.wait_ge(weight_act, 1)
            step(dve.tensor_tensor(out=by_block(sm(3)), in0=by_block(sm(1)), in1=per_block(sm(2)), op=ALU.mult))
            first = by_block(sm(3))[:, :, 0:1].to_broadcast([P, BLOCKS, TOP])
            step(dve.tensor_tensor(out=by_block(sm(2)), in0=by_block(sm(3)), in1=first, op=ALU.subtract))
            dve.wait_ge(weight_act, 2)
            step(dve.tensor_reduce(sm(3)[:, 0:BLOCKS], by_block(sm(1)), AX_X, ALU.add))
            step(dve.reciprocal(sm(3)[:, 0:BLOCKS], sm(3)[:, 0:BLOCKS]))
            step(dve.tensor_tensor(out=by_block(sm(2)), in0=by_block(sm(1)), in1=per_block(sm(3)), op=ALU.mult))

            mixes = [0]

            def mix(ins):
                mixes[0] += 1
                ins.then_inc(mix_step, 1)
                dve.wait_ge(mix_step, mixes[0])

            dve.wait_ge(x_again, 16)
            for j in range(BLOCKS):
                dve.wait_ge(gathered[j], 16 * TOP)
            xr = by_block(plane_x[:, :], P)
            prod = by_block(pair[:, 0:N], P)
            for k in range(TOP):
                wk_b = by_block(sm(2))[:, :, k:k + 1].to_broadcast([P, BLOCKS, P])
                mix(dve.tensor_tensor(out=prod, in0=gather_v[:, :, k, :], in1=wk_b, op=ALU.mult))
                mix(dve.tensor_tensor(out=xr, in0=xr, in1=prod, op=ALU.add))
            mix(dve.tensor_reduce(sm(4)[:, 0:BLOCKS], xr, AX_X, ALU.add))
            mix(dve.tensor_scalar(sm(4)[:, 0:BLOCKS], sm(4)[:, 0:BLOCKS], 1.0 / P, None, ALU.mult))
            mix(dve.tensor_tensor(out=xr, in0=xr, in1=per_block(sm(4), P), op=ALU.subtract))
            dve.wait_ge(mix_act, 1)
            mix(dve.tensor_reduce(sm(4)[:, 0:BLOCKS], prod, AX_X, ALU.add))
            mix(dve.tensor_scalar(sm(4)[:, 0:BLOCKS], sm(4)[:, 0:BLOCKS], 1.0 / P, 1e-5, ALU.mult, ALU.add))
            dve.wait_ge(mix_act, 2)
            mix(dve.reciprocal(sm(6)[:, 0:BLOCKS], sm(5)[:, 0:BLOCKS]))
            mix(dve.tensor_tensor(out=sm(6)[:, 0:BLOCKS], in0=sm(6)[:, 0:BLOCKS], in1=sm(4)[:, 0:BLOCKS], op=ALU.mult))
            mix(dve.tensor_tensor(out=sm(6)[:, 0:BLOCKS], in0=sm(6)[:, 0:BLOCKS], in1=sm(5)[:, 0:BLOCKS], op=ALU.add))
            mix(dve.tensor_scalar(sm(6)[:, 0:BLOCKS], sm(6)[:, 0:BLOCKS], 0.5, None, ALU.mult))
            mix(dve.reciprocal(sm(6)[:, 0:BLOCKS], sm(6)[:, 0:BLOCKS]))
            dve.tensor_tensor(out=xr, in0=xr, in1=per_block(sm(6), P), op=ALU.mult).then_inc(x1_ready, 1)
            for g in range(TILES):
                dve.wait_ge(x1_turned, g + 1)
                dve.tensor_copy(plane_y[:, g * TW:(g + 1) * TW], bank(g)).then_inc(x1_cols, 1)
            dve.wait_ge(x1_cols, TILES)

            for b in range(LAYERS):
                with dve.Fori(0, TILES) as t:
                    dve.wait_ge(a_kept[b], t + 1)
                    dve.tensor_scalar(a_cols[:, tile(t)], stage[:, :], 1.0, None, ALU.mult).then_inc(a_rows[b], 1)
                    dve.wait_ge(a_turned[b], t + 1)
                    dve.tensor_scalar(a_rows_v[:, tile(t)], bank(6), 1.0, None, ALU.mult).then_inc(a_rows[b], 1)
                with dve.Fori(0, TILES) as t:
                    dve.wait_ge(chunk_used, CHUNKS * (TILES * (2 + 2 * b) + 1) + t * CHUNKS)
                    dve.wait_ge(mix_ready[b], CREDIT + t)
                    if b == LAYERS - 1:
                        dve.wait_ge(row_out, CREDIT + t)
                    dve.scalar_tensor_tensor(out=stage[:, :], in0=ps[:, tile(t)], scalar=2.0, in1=z_cols[b][:, tile(t)],
                                             op0=ALU.mult, op1=ALU.subtract).then_inc(t2_kept[b], 1)
                    dve.wait_ge(mix_ready[b], CREDIT + t + 1)
                    dve.wait_ge(pos_kept[b], t + 1)
                    dve.tensor_scalar(tmp_b[:, :], bank(7), chebb_s[:, b:b + 1], 0.0, ALU.add, ALU.min).then_inc(
                        neg_kept[b], 1)
                    dve.wait_ge(exp_kept[b], t + 1)
                    dve.scalar_tensor_tensor(out=tmp_a[:, :], in0=tmp_b[:, :], scalar=-1.0, in1=tmp_a[:, :],
                                             op0=ALU.add, op1=ALU.add).then_inc(h_kept[b], 1)
                    if b == 0:
                        dve.wait_ge(h_kept[b], CREDIT + t + 1)
                        dve.tensor_scalar(z_cols[1][:, tile(t)], tmp_a[:, :], 1.0, None, ALU.mult)
                        dve.wait_ge(h_turned[b], t + 1)
                        dve.tensor_scalar(z_rows[1][:, tile(t)], bank(6), 1.0, None, ALU.mult).then_inc(h_rows[b], 1)
                    else:
                        rows = stage[:, :].rearrange("p (q d) -> p q d", d=P)

                        def per_row(i):
                            return sm(i)[:, 0:BPT].unsqueeze(2).to_broadcast([P, BPT, P])

                        dve.wait_ge(h_turned[b], t + 1)
                        dve.tensor_tensor(out=stage[:, :], in0=bank(6), in1=plane_x[:, tile(t)], op=ALU.add).then_inc(
                            ln_step, 1)
                        dve.wait_ge(ln_step, 8 * t + 1)
                        dve.tensor_reduce(sm(3)[:, 0:BPT], rows, AX_X, ALU.add).then_inc(ln_step, 1)
                        dve.wait_ge(ln_step, 8 * t + 2)
                        dve.tensor_scalar(sm(3)[:, 0:BPT], sm(3)[:, 0:BPT], 1.0 / P, None, ALU.mult).then_inc(h_rows[b], 1)
                        dve.wait_ge(h_rows[b], CREDIT + t + 1)
                        dve.wait_ge(stored, CREDIT + 16 * t)
                        dve.tensor_tensor(out=rows, in0=rows, in1=per_row(3), op=ALU.subtract).then_inc(ln_step, 1)
                        dve.wait_ge(ln_act, 2 * t + 1)
                        dve.tensor_reduce(sm(4)[:, 0:BPT], tmp_c[:, :].rearrange("p (q d) -> p q d", d=P), AX_X,
                                          ALU.add).then_inc(ln_step, 1)
                        dve.wait_ge(ln_step, 8 * t + 4)
                        dve.tensor_scalar(sm(4)[:, 0:BPT], sm(4)[:, 0:BPT], 1.0 / P, 1e-5, ALU.mult,
                                          ALU.add).then_inc(ln_step, 1)
                        dve.wait_ge(ln_act, 2 * t + 2)
                        dve.reciprocal(sm(6)[:, 0:BPT], sm(5)[:, 0:BPT]).then_inc(ln_step, 1)
                        dve.wait_ge(ln_step, 8 * t + 6)
                        dve.scalar_tensor_tensor(out=sm(6)[:, 0:BPT], in0=sm(6)[:, 0:BPT], scalar=1.0,
                                                 in1=sm(4)[:, 0:BPT], op0=ALU.mult, op1=ALU.mult).then_inc(ln_step, 1)
                        dve.wait_ge(ln_step, 8 * t + 7)
                        dve.tensor_tensor(out=sm(6)[:, 0:BPT], in0=sm(6)[:, 0:BPT], in1=sm(5)[:, 0:BPT],
                                          op=ALU.add).then_inc(ln_step, 1)
                        dve.wait_ge(ln_step, 8 * t + 8)
                        dve.reciprocal(sm(5)[:, 0:BPT], sm(6)[:, 0:BPT]).then_inc(root_kept, 1)
                        dve.wait_ge(root_kept, t + 1)
                        dve.scalar_tensor_tensor(out=tmp_c[:, :].rearrange("p (q d) -> p q d", d=P), in0=rows,
                                                 scalar=2.0, in1=per_row(5), op0=ALU.mult, op1=ALU.mult).then_inc(
                                                     row_out, 1)
                if b == 0:
                    dve.wait_ge(h_rows[b], CREDIT + TILES)


def kernel(x, adj, L0_gnn_w_h, L0_gnn_w_hf, L0_gnn_wq, L0_gnn_wk, L0_gnn_wv, L0_gnn_ffn_w, L0_gnn_ffn_b,
           L1_gnn_W0, L1_gnn_b0, L1_gnn_W1, L1_gnn_b1):
    import numpy as np
    import concourse.bacc as bacc
    from concourse.bass_utils import run_bass_kernel_spmd

    def rows(a):
        a = np.asarray(a)
        return a.reshape(-1, P, a.shape[-1]).transpose(1, 0, 2).reshape(P, -1)

    def doubled(w):
        w = np.asarray(w).transpose(2, 0, 1).reshape(P, LAYERS, HEADS, 1, DH)
        return np.concatenate([w, w], axis=3).reshape(P, -1)

    def side(w):
        return np.asarray(w).transpose(2, 0, 1).reshape(P, -1)

    adj_t = np.asarray(adj).reshape(TILES, TW, BLOCKS, P).transpose(3, 0, 2, 1).reshape(P, -1)
    cheb = np.concatenate([np.asarray(L1_gnn_W0), np.asarray(L1_gnn_W1)], axis=0)
    arrays = {
        "x_rows": rows(x),
        "x_cols": np.asarray(x).T,
        "adj_t": adj_t,
        "w_h": np.asarray(L0_gnn_w_h).T,
        "w_hf": np.asarray(L0_gnn_w_hf).T,
        "wq": doubled(L0_gnn_wq),
        "wk": doubled(L0_gnn_wk),
        "wv": side(L0_gnn_wv),
        "ffn_w": side(L0_gnn_ffn_w),
        "ffn_b": np.asarray(L0_gnn_ffn_b).T,
        "cheb_w": cheb.transpose(1, 0, 2).reshape(P, -1),
        "cheb_b": np.stack([np.asarray(L1_gnn_b0), np.asarray(L1_gnn_b1)], axis=1),
    }
    arrays = {k: np.ascontiguousarray(v) for k, v in arrays.items()}
    nc = bacc.Bacc("TRN2", target_bir_lowering=False, num_devices=1)
    args = [nc.dram_tensor(f"in_{k}", v.shape, F32, kind="ExternalInput").ap() for k, v in arrays.items()]
    out = nc.dram_tensor("out_rows", (P, N), F32, kind="ExternalOutput").ap()
    gnn_kernel(nc, *args, out)
    r = run_bass_kernel_spmd(nc, [{f"in_{k}": v for k, v in arrays.items()}], core_ids=[0])
    got = r.results[0]["out_rows"]
    return np.ascontiguousarray(got.reshape(P, BLOCKS, P).transpose(1, 0, 2).reshape(N, P))
```

```python
from contextlib import ExitStack

import concourse.bass as bass
from concourse import mybir

P = 128
F32 = mybir.dt.float32
F32R = mybir.dt.float32r
BF16 = mybir.dt.bfloat16
U32 = mybir.dt.uint32
ALU = mybir.AluOpType
ACT = mybir.ActivationFunctionType
AX_X = mybir.AxisListType.X

N = 3072
TW = 512
TILES = N // TW
BLOCKS = N // P
BPT = TW // P
CH = 2
CW = CH * TW
CHUNKS = BLOCKS // CH
RAWS = 6
SPLITS = 4
HEADS = 2
DH = P // HEADS
LAYERS = 2
SLOTS = 3
BANKS = 8
TOP = 3
GATHERS = 10
CREDIT = 1
KB = 1024


def tile(t, shift=0):
    return bass.ds((t + shift) * TW, TW)


def cols(ap, n=P):
    return ap.rearrange("p (j k) -> p j k", k=n)


def gnn_kernel(nc, x_rows_d, x_cols_d, adj_t, w_h, w_hf, wq, wk, wv, ffn_w, ffn_b, cheb_w, cheb_b, out):
    with ExitStack() as ctx:
        def sb(name, width, dt=F32):
            return ctx.enter_context(nc.sbuf_tensor(name, [P, width], dt))

        def sem(name):
            return ctx.enter_context(nc.semaphore(name))

        def sems(name, n):
            return [sem(f"{name}{i}") for i in range(n)]

        ps = ctx.enter_context(nc.psum_tensor("ps", [P, BANKS * TW], F32))

        def bank(k):
            return ps[:, k * TW:(k + 1) * TW]

        plane_x = sb("plane_x", N)
        plane_y = sb("plane_y", N + TW)
        wh_s = sb("wh_s", 3 * P)
        whf_s = sb("whf_s", 2 * P)
        wq_s = sb("wq_s", LAYERS * P)
        wk_s = sb("wk_s", LAYERS * P)
        wv_s = sb("wv_s", LAYERS * P)
        ffn_s = sb("ffn_s", LAYERS * P)
        ffnb_s = sb("ffnb_s", LAYERS)
        cheb_s = sb("cheb_s", LAYERS * 3 * P)
        chebb_s = sb("chebb_s", LAYERS)
        ident = sb("ident", P)
        gram = sb("gram", 2 * P)
        half_power = sb("half_power", 1)
        sum_stage = sb("sum_stage", TW)
        y_stage = sb("y_stage", TW)
        relu_stage = sb("relu_stage", TW)
        exp_stage = sb("exp_stage", TW)
        turn_stage = sb("turn_stage", TW)
        out_stage = sb("out_stage", TW)
        block_split = [sb(f"block_split{i}", 2 * P, F32R) for i in range(2)]
        top_v = sb("top_v", BLOCKS * 8)
        top_i = sb("top_i", BLOCKS * 8, U32)
        squares = sb("squares", BLOCKS)
        inv_norm = sb("inv_norm", BLOCKS)
        exp_sum = sb("exp_sum", BLOCKS)
        weight_e = sb("weight_e", BLOCKS * TOP)
        weight_p = sb("weight_p", BLOCKS * TOP)
        weight = sb("weight", BLOCKS * TOP)
        stats = sb("stats", BPT * 6)
        mean_var = sb("mean_var", BPT * 2)
        var_eps = sb("var_eps", BPT)
        inv_std = sb("inv_std", BPT)

        base = -(-nc.sbuf_base // 32) * 32

        def at(name, kb, width, dt=F32):
            return nc.alloc_sbuf_tensor_at(name, [P, width], dt, offset=base + kb * KB)

        k_split = [[at(f"k_split{b}{h}", 36 * b + 12 * h, N, F32R) for h in range(HEADS)] for b in range(LAYERS)]
        v_rows = [at(f"v_rows{b}", 36 * b + 24, N) for b in range(LAYERS)]
        xh = cols(at("xh", 36, 2 * N)[:, :], 2 * P)
        raws_front = [at(f"raw_front{i}", 60 + 4 * i, CW) for i in range(RAWS)]
        hi_front = [at(f"hi_front{i}", 84 + 4 * i, CW, F32R) for i in range(SPLITS)]
        lo_front = [at(f"lo_front{i}", 100 + 4 * i, CW, F32R) for i in range(SPLITS)]
        h0_hi, h0_lo = at("h0_hi", 116, N, F32R), at("h0_lo", 128, N, F32R)
        q_hi = [at(f"q_hi{h}", 72 + 28 * h, N + TW, F32R) for h in range(HEADS)]
        q_lo = [at(f"q_lo{h}", 86 + 28 * h, N + TW, F32R) for h in range(HEADS)]
        probs_all = at("probs", 128, SLOTS * HEADS * TW)
        probs = [probs_all[:, s * HEADS * TW:(s + 1) * HEADS * TW] for s in range(SLOTS)]
        y_rows = at("y_rows", 0, N)
        unit_hi, unit_lo = at("unit_hi", 12, N, F32R), at("unit_lo", 24, N, F32R)
        cos_rows = [at(f"cos_rows{i}", 36 + 12 * i, N) for i in range(2)]
        gather = cols(at("gather", 60, GATHERS * TOP * P)[:, :])
        exp_dump = at("exp_dump", 75, N, BF16)
        hi_cheb = [at(f"hi_cheb{i}", 81 + 4 * i, CW, F32R) for i in range(SPLITS)]
        lo_cheb = [at(f"lo_cheb{i}", 97 + 4 * i, CW, F32R) for i in range(SPLITS)]
        z_hi, z_lo = at("z_hi", 113, N, F32R), at("z_lo", 125, N, F32R)
        raws_cheb = [at(f"raw_cheb{i}", (0 if i < 3 else 125) + 4 * i, CW) for i in range(RAWS)]
        a_cols = at("a_cols", 12, N)
        a_hi, a_lo = at("a_hi", 36, N, F32R), at("a_lo", 48, N, F32R)
        assert base + 149 * KB <= nc.sbuf_usable_end

        y_dram = nc.dram_tensor("y_scratch", [N, P], F32)

        loaded_first, loaded = sem("loaded_first"), sem("loaded")
        consts_set, ident_set = sem("consts_set"), sem("ident_set")
        adj_in = sems("adj_in", RAWS)
        hi_kept, lo_kept, chunk_used = sem("hi_kept"), sem("lo_kept"), sem("chunk_used")
        h0_ready, h0_split, h0_kept = sem("h0_ready"), sem("h0_split"), sem("h0_kept")
        gram_ready, gram_kept = sem("gram_ready"), sem("gram_kept")
        uc_ready, uc_squared, uc_summed, uc_kept = sem("uc_ready"), sem("uc_squared"), sem("uc_summed"), sem("uc_kept")
        norm_kept, corr_scaled, corr_turned, corr_kept = (
            sem("norm_kept"), sem("corr_scaled"), sem("corr_turned"), sem("corr_kept"))
        agg_kept, gate_ready, gate_relu, gated = sem("agg_kept"), sem("gate_ready"), sem("gate_relu"), sem("gated")
        h2_ready, y0_kept, y0_cols = sem("h2_ready"), sem("y0_kept"), sem("y0_cols")
        kv_ready, k0_hi, k0_lo, v0_kept = sem("kv_ready"), sem("k0_hi"), sem("k0_lo"), sem("v0_kept")
        scores_ready, tanh_done, probs_used = sem("scores_ready"), sem("tanh_done"), sem("probs_used")
        att_kept = sem("att_kept")
        side_ready, side_done = sem("side_ready"), sem("side_done")
        relu_kept, k_hi_kept, q_hi_kept = sem("relu_kept"), sem("k_hi_kept"), sem("q_hi_kept")
        y_squared = sem("y_squared")
        y_out, x_again = sem("y_out"), sem("x_again")
        sum_eps, fl_kept = sem("sum_eps"), sem("fl_kept")
        unit_staged, unit_turned = sem("unit_staged"), sem("unit_turned")
        unit_hi_kept, unit_lo_kept = sem("unit_hi_kept"), sem("unit_lo_kept")
        block_staged, cos_ready, cos_kept = sem("block_staged"), sem("cos_ready"), sem("cos_kept")
        exp_done, top_done, index_done = sem("exp_done"), sem("top_done"), sem("index_done")
        gathered = sems("gathered", BLOCKS)
        weight_exp, weight_diff, weight_step, weight_kept = (
            sem("weight_exp"), sem("weight_diff"), sem("weight_step"), sem("weight_kept"))
        mix_step, mixed = sem("mix_step"), sem("mixed")
        ln_step, ln_var, ln_power = sem("ln_step"), sem("ln_var"), sem("ln_power")
        x1_kept, x1_hi, x1_lo = sem("x1_kept"), sem("x1_hi"), sem("x1_lo")
        x1_staged, x1_turned, x1_cols = sem("x1_staged"), sem("x1_turned"), sem("x1_cols")
        a_staged, a_turned, a_cols_kept = sem("a_staged"), sem("a_turned"), sem("a_cols_kept")
        a_hi_kept, a_lo_kept = sem("a_hi_kept"), sem("a_lo_kept")
        t2_kept, mix_ready, pos_kept, neg_kept, exp_kept = (
            sem("t2_kept"), sem("mix_ready"), sem("pos_kept"), sem("neg_kept"), sem("exp_kept"))
        h_staged, h_turned, h_hi_kept, h_lo_kept = sem("h_staged"), sem("h_turned"), sem("h_hi_kept"), sem("h_lo_kept")
        row_out, stored, out_free = sem("row_out"), sem("stored"), sem("out_free")

        start_values = {
            lo_kept: RAWS, chunk_used: SPLITS,
            tanh_done: SLOTS, probs_used: SLOTS, cos_kept: BANKS, index_done: 2, exp_done: 2,
            gate_ready: CREDIT, k0_lo: CREDIT, kv_ready: CREDIT, y0_kept: CREDIT, y0_cols: CREDIT, att_kept: CREDIT,
            x1_turned: CREDIT, x1_cols: CREDIT, a_turned: CREDIT, a_cols_kept: CREDIT, a_lo_kept: CREDIT,
            mix_ready: CREDIT, h_staged: CREDIT, h_turned: CREDIT, h_lo_kept: CREDIT, out_free: CREDIT,
        }

        def job_f(b, tau):
            return 2 + 4 * tau if b == 0 else 27 + 3 * tau

        first_q = [0, 22]
        last_f0 = 23

        block = ctx.enter_context(nc.Block())

        def chunk_no(n_pass, t, c):
            return CHUNKS * TILES * n_pass + c + t * CHUNKS

        def tile_done(n_pass, tau):
            return SPLITS + CHUNKS * (TILES * n_pass + 1) + tau * CHUNKS

        def raw_slots(n_pass):
            return raws_front if n_pass == 0 else raws_cheb

        @block.sync
        def _(sp):
            def load(n_pass, t, c):
                sp.wait_ge(lo_kept, chunk_no(n_pass, t, c) + 1)
                sp.dma_start(raw_slots(n_pass)[c % RAWS][:, :],
                             adj_t[:, bass.ds(t * (BLOCKS * TW) + c * CW, CW)]).then_inc(adj_in[c % RAWS], 16)

            sp.dma_start(plane_x[:, :], x_cols_d).then_inc(loaded_first, 16)
            sp.dma_start(wh_s[:, :], w_h).then_inc(loaded_first, 16)
            sp.dma_start(xh[:, :, 0:P], cols(x_rows_d)).then_inc(loaded_first, 16)
            for n_pass in range(1 + 2 * LAYERS):
                if n_pass == 1:
                    sp.wait_ge(y_out, 16)
                    sp.wait_ge(unit_staged, TILES)
                with sp.Fori(0, TILES) as t:
                    for c in range(CHUNKS):
                        load(n_pass, t, c)

        @block.gpsimd
        def _(pool):
            for s, v in start_values.items():
                pool.sem_inc(s, v)
            pool.memset(half_power[:, :], -0.5).then_inc(consts_set, 1)
            pool.memset(ident[:, :], 0.0).then_inc(ident_set, 1)
            pool.wait_ge(ident_set, 1)
            pool.affine_select(out=ident[:, :], in_=ident[:, :], compare_op=ALU.not_equal, fill=1.0, base=0,
                               pattern=[[-1, P]], channel_multiplier=1).then_inc(ident_set, 1)
            pool.memset(plane_y[:, N:N + TW], 0.0).then_inc(consts_set, 1)

            def inv_root(dst, src, width):
                return pool.tensor_tensor(out=dst, in0=src, in1=half_power[:, 0:1].to_broadcast([P, width]),
                                          op=ALU.pow)

            pool.wait_ge(consts_set, 2)
            pool.wait_ge(uc_summed, BLOCKS // 2)
            inv_root(inv_norm[:, :], squares[:, :], BLOCKS).then_inc(norm_kept, 1)

            pool.wait_ge(side_done, job_f(1, TILES - 1) + 2)
            pool.dma_start(y_dram[:, :].rearrange("(j p) d -> p j d", p=P), cols(y_rows[:, :])).then_inc(y_out, 16)
            pool.wait_ge(sum_eps, 1)
            inv_root(inv_norm[:, :], squares[:, :], BLOCKS).then_inc(fl_kept, 1)

            def stage_block(j):
                dst = block_split[j % 2]
                if j < 2:
                    pool.wait_ge(unit_lo_kept, 1)
                else:
                    pool.wait_ge(cos_ready, TILES * (j - 1))
                pool.tensor_copy(dst[:, 0:P], unit_hi[:, j * P:(j + 1) * P].bitcast(F32))
                pool.tensor_copy(dst[:, P:2 * P], unit_lo[:, j * P:(j + 1) * P].bitcast(F32)).then_inc(block_staged, 1)

            mixes = 0
            stage_block(0)
            stage_block(1)
            pool.wait_ge(y_out, 16)
            for j in range(BLOCKS + 9):
                if j + 2 < BLOCKS:
                    stage_block(j + 2)
                q = (j - 11) // BPT
                if (j - 11) % BPT == 0 and 0 <= q < TILES:
                    pool.wait_ge(ln_var, q + 1)
                    inv_root(inv_std[:, :], var_eps[:, :], BPT).then_inc(ln_power, 1)
                if j < BLOCKS:
                    pool.wait_ge(index_done, 2 + j + 1)
                    for k in range(TOP):
                        pool.indirect_dma_start(
                            gather[:, (j % GATHERS) * TOP + k, :], None, y_dram[:, :],
                            bass.IndirectOffsetOnAxis(ap=top_i[:, j * 8 + k:j * 8 + k + 1], axis=0),
                        ).then_inc(gathered[j], 16)
                q = (j - 9) // BPT
                if (j - 9) % BPT == 0 and 0 <= q < TILES:
                    pool.wait_ge(weight_kept, q + 1)
                    if q == 0:
                        pool.wait_ge(x_again, 16)
                    for m in range(BPT * q, BPT * (q + 1)):
                        pool.wait_ge(gathered[m], 16 * TOP)
                        xm = plane_x[:, m * P:(m + 1) * P]
                        for k in range(TOP):
                            w = weight[:, m * TOP + k:m * TOP + k + 1]
                            pool.tensor_scalar(exp_stage[:, k * P:(k + 1) * P], gather[:, (m % GATHERS) * TOP + k, :],
                                               w, 1.0, ALU.mult, ALU.mult).then_inc(mix_step, 1)
                        for k in range(TOP):
                            pool.wait_ge(mix_step, mixes + TOP + k)
                            s = mixed if k == TOP - 1 else mix_step
                            pool.tensor_tensor(out=xm, in0=xm, in1=exp_stage[:, k * P:(k + 1) * P],
                                               op=ALU.add).then_inc(s, 1)
                        mixes += 2 * TOP - 1
                        pool.wait_ge(mixed, m + 1)

            with pool.Fori(0, TILES) as t:
                pool.wait_ge(x1_kept, t + 1)
                pool.wait_ge(x1_turned, CREDIT + t)
                pool.tensor_copy(turn_stage[:, :], plane_x[:, tile(t)]).then_inc(x1_staged, 1)
            with pool.Fori(0, TILES) as t:
                pool.wait_ge(ln_var, TILES + 1 + t)
                inv_root(inv_std[:, :], var_eps[:, :], BPT).then_inc(ln_power, 1)
                pool.wait_ge(row_out, t + 1)
                pool.dma_start(out[:, tile(t)], out_stage[:, :]).then_inc(stored, 16)
                pool.wait_ge(stored, 16 * t + 16)
                pool.sem_inc(out_free, 1)

        @block.scalar
        def _(act):
            for dst, src in ((whf_s, w_hf), (wq_s, wq), (wk_s, wk), (wv_s, wv), (ffn_s, ffn_w), (ffnb_s, ffn_b),
                             (cheb_s, cheb_w), (chebb_s, cheb_b)):
                act.dma_start(dst[:, :], src).then_inc(loaded, 16)

            def copy(dst, src):
                return act.activation(dst, src, ACT.Copy)

            def high_part(n_pass, t, c, his):
                act.wait_ge(adj_in[c % RAWS], 16 * (2 * TILES * n_pass + c // RAWS + 1) + t * 32)
                act.wait_ge(chunk_used, chunk_no(n_pass, t, c) + 1)
                copy(his[c % SPLITS][:, :], raw_slots(n_pass)[c % RAWS][:, :]).then_inc(hi_kept, 1)

            for g in range(TILES):
                act.wait_ge(h0_ready, g + 1)
                copy(h0_hi[:, g * TW:(g + 1) * TW], bank(g)).then_inc(h0_split, 1)
            act.wait_ge(gram_ready, 1)
            copy(gram[:, :], bank(6)[:, 0:2 * P]).then_inc(gram_kept, 1)
            for i in range(BLOCKS // 2):
                act.wait_ge(uc_squared, i + 1)
                copy(xh[:, 2 * i:2 * i + 2, P:2 * P], cols(bank(i % 6), 2 * P)[:, :, P:2 * P]).then_inc(uc_kept, 1)

            def gate_relu_of(tau):
                act.wait_ge(gate_ready, 2 * tau + CREDIT + 1)
                act.wait_ge(y0_kept, CREDIT + tau)
                act.activation(relu_stage[:, :], ps[:, tile(tau)], ACT.Relu).then_inc(gate_relu, 1)

            def y0_of(tau):
                act.wait_ge(y0_kept, CREDIT + tau + 1)
                copy(plane_y[:, tile(tau)], y_stage[:, :]).then_inc(y0_cols, 1)

            def kv0_of(tau):
                act.wait_ge(kv_ready, 2 * tau + CREDIT + 1)
                for h in range(HEADS):
                    copy(k_split[0][h][0:DH, tile(tau)], bank(7)[h * DH:(h + 1) * DH, :]).then_inc(k0_hi, 1)
                act.wait_ge(kv_ready, 2 * tau + CREDIT + 2)
                copy(v_rows[0][:, tile(tau)], ps[:, tile(tau)]).then_inc(v0_kept, 1)

            for c in range(CHUNKS):
                high_part(0, 0, c, hi_front)
                if c >= 6:
                    i = c - 6
                    act.wait_ge(corr_turned, i + 1)
                    copy(plane_y[:, i * TW:(i + 1) * TW], bank(2 + i)).then_inc(corr_kept, 1)
            with act.Fori(1, TILES) as t:
                for c in range(CHUNKS):
                    high_part(0, t, c, hi_front)
                    if c == 6:
                        gate_relu_of(t - 1)
                    if c == 10:
                        y0_of(t - 1)
                    if c == 11:
                        kv0_of(t - 1)
            gate_relu_of(TILES - 1)
            y0_of(TILES - 1)
            kv0_of(TILES - 1)

            def relu_of(b, tau, job):
                act.wait_ge(side_ready, job + 1)
                act.activation(relu_stage[:, :], bank(7), ACT.Relu, bias=ffnb_s[:, b:b + 1]).then_inc(relu_kept, 1)

            def k_hi_of(tau, job):
                act.wait_ge(side_ready, job + 1)
                for h in range(HEADS):
                    copy(k_split[1][h][0:DH, tile(tau)], bank(7)[h * DH:(h + 1) * DH, :]).then_inc(k_hi_kept, 1)

            def q_hi_of(t, job):
                act.wait_ge(side_ready, job + 1)
                for h in range(HEADS):
                    for z in range(2):
                        copy(q_hi[h][z * DH:(z + 1) * DH, tile(t)],
                             bank(7)[h * DH:(h + 1) * DH, :]).then_inc(q_hi_kept, 1)

            def tanh_tile(b, t, after):
                for g in range(BLOCKS):
                    s = g % SLOTS
                    act.wait_ge(scores_ready, BLOCKS * (TILES * b + t) + g + 1)
                    act.wait_ge(probs_used, BLOCKS * (TILES * b + t) + g + 1)
                    act.activation(probs[s], ps[:, HEADS * s * TW:HEADS * (s + 1) * TW], ACT.Tanh).then_inc(
                        tanh_done, 1)
                    after(g)

            for b in range(LAYERS):
                q_hi_of(0, first_q[b])

                def first(g):
                    if b and g == 5:
                        relu_of(0, TILES - 1, last_f0)
                    if b and g == 9:
                        k_hi_of(TILES - 1, last_f0 + 1)
                    if g == 18:
                        q_hi_of(1, 1 if b == 0 else last_f0 + 3)

                tanh_tile(b, 0, first)
                with act.Fori(1, TILES) as t:
                    def later(g):
                        f = job_f(b, t - 1)
                        if g == 5:
                            relu_of(b, t - 1, f)
                        if b == 0 and g == 9:
                            k_hi_of(t - 1, f + 1)
                        if g == 18:
                            q_hi_of(t + 1, f + (3 if b == 0 else 2))

                    tanh_tile(b, t, later)
                if b == 0:
                    act.dma_start(plane_x[:, :], x_rows_d).then_inc(x_again, 16)
            relu_of(1, TILES - 1, job_f(1, TILES - 1))

            for t in range(TILES):
                act.wait_ge(unit_turned, t + 1)
                copy(unit_hi[:, t * TW:(t + 1) * TW], bank(t)).then_inc(unit_hi_kept, 1)

            def cos_block(q, i):
                for n in range(TILES):
                    u = TILES * i + n
                    act.wait_ge(cos_ready, BPT * TILES * q + u + 1)
                    if n == 0:
                        act.wait_ge(index_done, BPT * q + i + 1)
                        act.wait_ge(exp_done, BPT * q + i + 1)
                    copy(cos_rows[i % 2][:, n * TW:(n + 1) * TW], bank(u % BANKS)).then_inc(cos_kept, 1)
                act.wait_ge(cos_kept, BANKS + BPT * TILES * q + TILES * (i + 1))
                act.wait_ge(exp_done, BPT * q + i + 2)
                act.activation(exp_dump[:, :], cos_rows[i % 2][:, :], ACT.Exp,
                               accum_out=exp_sum[:, bass.ds(BPT * q + i, 1)]).then_inc(exp_done, 1)

            def top_exp(q):
                act.wait_ge(top_done, BPT * q + BPT)
                act.activation(cols(weight_e[:, :], TOP)[:, bass.ds(BPT * q, BPT), :],
                               cols(top_v[:, :], 8)[:, bass.ds(BPT * q, BPT), 0:TOP], ACT.Exp).then_inc(weight_exp, 1)

            def diff_exp(q):
                act.wait_ge(weight_diff, q + 1)
                w = weight_e[:, bass.ds(q * (BPT * TOP), BPT * TOP)]
                act.activation(w, w, ACT.Exp).then_inc(weight_exp, 1)

            act.wait_ge(unit_lo_kept, TILES)
            for i in range(BPT):
                cos_block(0, i)
            with act.Fori(1, TILES) as q:
                for i in range(BPT):
                    cos_block(q, i)
                    if i == 1:
                        top_exp(q - 1)
                    if i == 3:
                        diff_exp(q - 1)
            top_exp(TILES - 1)
            diff_exp(TILES - 1)

            def a_stage_of(b, tau):
                act.wait_ge(chunk_used, tile_done(1 + 2 * b, tau))
                act.wait_ge(a_turned, CREDIT + TILES * b + tau)
                act.wait_ge(a_cols_kept, CREDIT + TILES * b + tau)
                copy(sum_stage[:, :], ps[:, tile(tau)]).then_inc(a_staged, 1)

            def a_hi_of(b, tau):
                act.wait_ge(a_turned, CREDIT + TILES * b + tau + 1)
                copy(a_hi[:, tile(tau)], bank(6)).then_inc(a_hi_kept, 1)

            def pos_of(b, tau):
                act.wait_ge(mix_ready, CREDIT + TILES * b + tau + 1)
                act.wait_ge(h_staged, CREDIT + TILES * b + tau)
                act.activation(relu_stage[:, :], bank(7), ACT.Relu, bias=chebb_s[:, b:b + 1]).then_inc(pos_kept, 1)

            def exp_of(b, tau):
                act.wait_ge(neg_kept, TILES * b + tau + 1)
                act.activation(exp_stage[:, :], exp_stage[:, :], ACT.Exp).then_inc(exp_kept, 1)

            def h_hi_of(tau):
                act.wait_ge(h_turned, CREDIT + tau + 1)
                copy(z_hi[:, tile(tau)], bank(6)).then_inc(h_hi_kept, 1)

            def chunk_steps(n_pass, t, c, what, b, tau):
                high_part(n_pass, t, c, hi_cheb)
                if what == "a" and c == 3:
                    a_stage_of(b, tau)
                if what == "a" and c == 6:
                    a_hi_of(b, tau)
                if what == "h" and c == 6:
                    pos_of(b, tau)
                if what == "h" and c == 7:
                    exp_of(b, tau)
                if what == "h" and c == 10 and b == 0:
                    h_hi_of(tau)
                if n_pass == 1 and c == 11:
                    act.wait_ge(x1_turned, CREDIT + t + 1)
                    copy(plane_y[:, tile(t)], bank(7)).then_inc(x1_cols, 1)

            for n_pass in range(1, 1 + 2 * LAYERS):
                b, half = (n_pass - 1) // 2, (n_pass - 1) % 2
                for c in range(CHUNKS):
                    if half:
                        chunk_steps(n_pass, 0, c, "a", b, TILES - 1)
                    else:
                        chunk_steps(n_pass, 0, c, "h" if b else "", b - 1, TILES - 1)
                with act.Fori(1, TILES) as t:
                    for c in range(CHUNKS):
                        chunk_steps(n_pass, t, c, "ah"[half], b, t - 1)
            pos_of(LAYERS - 1, TILES - 1)
            exp_of(LAYERS - 1, TILES - 1)

        @block.tensor
        def _(pe):
            def adj_chunk(n_pass, t, c, zh, zl, his, los):
                pe.wait_ge(lo_kept, RAWS + chunk_no(n_pass, t, c) + 1)
                hi, lo = his[c % SPLITS], los[c % SPLITS]
                for i in range(CH):
                    j = c * CH + i
                    zj = slice(j * P, (j + 1) * P)
                    part = slice(i * TW, (i + 1) * TW)
                    dst = ps[:, tile(t)]
                    pe.matmul(dst, zh[:, zj], hi[:, part], start=(j == 0), stop=False)
                    pe.matmul(dst, zh[:, zj], lo[:, part], start=False, stop=False)
                    mm = pe.matmul(dst, zl[:, zj], hi[:, part], start=False, stop=(j == BLOCKS - 1))
                mm.then_inc(chunk_used, 1)

            def turn(dst, src):
                for q in range(BPT):
                    mm = pe.transpose(dst[:, q * P:(q + 1) * P], src[:, q * P:(q + 1) * P], ident[:, :])
                return mm

            pe.wait_ge(loaded_first, 16 * 3)
            for j in range(BLOCKS):
                mm = pe.matmul(ps[:, j * P:(j + 1) * P], plane_x[:, j * P:(j + 1) * P], wh_s[:, 0:P],
                               start=True, stop=True)
                if j % BPT == BPT - 1:
                    mm.then_inc(h0_ready, 1)
            for j in range(BLOCKS):
                if j % BPT == 0:
                    pe.wait_ge(h0_kept, j // BPT + 1)
                mm = pe.matmul(bank(6)[:, 0:2 * P], xh[:, j, 0:P], xh[:, j, :], start=(j == 0), stop=(j == BLOCKS - 1))
            mm.then_inc(gram_ready, 1)
            pe.wait_ge(gram_kept, 1)
            for i in range(BLOCKS // 2):
                if i >= 6:
                    pe.wait_ge(uc_kept, i - 5)
                for k in range(2):
                    j = 2 * i + k
                    mm = pe.matmul(bank(i % 6)[:, k * 2 * P:(k + 1) * 2 * P], plane_x[:, j * P:(j + 1) * P], gram[:, :],
                                   start=True, stop=True)
                mm.then_inc(uc_ready, 1)

            def gate_of(tau):
                pe.wait_ge(agg_kept, tau + 1)
                pe.matmul(ps[:, tile(tau)], wh_s[:, P:2 * P], plane_x[:, tile(tau)], start=True, stop=False)
                pe.matmul(ps[:, tile(tau)], whf_s[:, 0:P], sum_stage[:, :], start=False, stop=True).then_inc(
                    gate_ready, 1)
                pe.wait_ge(k0_lo, 2 * tau + CREDIT)
                pe.matmul(bank(7), whf_s[:, P:2 * P], sum_stage[:, :], start=True, stop=True).then_inc(gate_ready, 1)

            def h2_of(tau):
                pe.wait_ge(gate_relu, tau + 1)
                pe.matmul(ps[:, tile(tau)], wh_s[:, 2 * P:3 * P], plane_x[:, tile(tau)], start=True,
                          stop=True).then_inc(h2_ready, 1)

            def kv0_of(tau):
                pe.wait_ge(y0_kept, CREDIT + tau + 1)
                pe.matmul(bank(7), wk_s[:, 0:P], y_stage[:, :], start=True, stop=True).then_inc(kv_ready, 1)
                for q in range(BPT):
                    mm = pe.matmul(ps[:, bass.ds(tau * TW + q * P, P)], y_stage[:, q * P:(q + 1) * P], wv_s[:, 0:P],
                                   start=True, stop=True)
                mm.then_inc(kv_ready, 1)

            front = (h0_hi, h0_lo, hi_front, lo_front)
            pe.wait_ge(uc_kept, BLOCKS // 2)
            pe.wait_ge(loaded, 16 * 8)
            pe.wait_ge(ident_set, 2)
            for c in range(CHUNKS):
                if c >= 6:
                    i = c - 6
                    pe.wait_ge(corr_scaled, i + 1)
                    for q in range(BPT):
                        mm = pe.transpose(bank(2 + i)[:, q * P:(q + 1) * P], xh[:, BPT * i + q, P:2 * P], ident[:, :])
                    mm.then_inc(corr_turned, 1)
                adj_chunk(0, 0, c, *front)
            pe.wait_ge(corr_kept, TILES)
            with pe.Fori(1, TILES) as t:
                for c in range(CHUNKS):
                    if c == 2:
                        gate_of(t - 1)
                    if c == 6:
                        h2_of(t - 1)
                    if c == 9:
                        kv0_of(t - 1)
                    adj_chunk(0, t, c, *front)
            gate_of(TILES - 1)
            h2_of(TILES - 1)
            kv0_of(TILES - 1)

            def score(b, t, g):
                pe.wait_ge(tanh_done, BLOCKS * (TILES * b + t) + g + 1)
                for h in range(HEADS):
                    dst = bank(HEADS * (g % SLOTS) + h)
                    kb = k_split[b][h][:, g * P:(g + 1) * P]
                    pe.matmul(dst, kb, q_hi[h][:, tile(t)], start=True, stop=False)
                    mm = pe.matmul(dst, kb, q_lo[h][:, tile(t)], start=False, stop=True)
                mm.then_inc(scores_ready, 1)

            def weigh(b, t, g):
                pe.wait_ge(tanh_done, SLOTS + BLOCKS * (TILES * b + t) + g + 1)
                for h in range(HEADS):
                    mm = pe.matmul(bank(6)[h * DH:(h + 1) * DH, :],
                                   v_rows[b][:, g * P + h * DH:g * P + (h + 1) * DH],
                                   probs[g % SLOTS][:, h * TW:(h + 1) * TW],
                                   start=(g == 0), stop=(g == BLOCKS - 1))
                mm.then_inc(probs_used, 1)

            def feed(b, tau, job):
                pe.wait_ge(att_kept, CREDIT + TILES * b + tau + 1)
                pe.wait_ge(side_done, job)
                pe.matmul(bank(7), ffn_s[:, b * P:(b + 1) * P], sum_stage[:, :], start=True, stop=True).then_inc(
                    side_ready, 1)

            def keys(job):
                pe.wait_ge(side_done, job)
                pe.matmul(bank(7), wk_s[:, P:2 * P], y_stage[:, :], start=True, stop=True).then_inc(side_ready, 1)

            def values(job):
                pe.wait_ge(side_done, job)
                for q in range(BPT):
                    mm = pe.matmul(bank(7)[:, q * P:(q + 1) * P], y_stage[:, q * P:(q + 1) * P], wv_s[:, P:2 * P],
                                   start=True, stop=True)
                mm.then_inc(side_ready, 1)

            def queries(b, t, job):
                if not (isinstance(job, int) and job == 0):
                    pe.wait_ge(side_done, job)
                pe.matmul(bank(7), wq_s[:, b * P:(b + 1) * P], plane_y[:, tile(t)], start=True, stop=True).then_inc(
                    side_ready, 1)

            def y_to_rows(job):
                pe.wait_ge(side_done, job)
                turn(bank(7), y_stage).then_inc(side_ready, 1)

            pe.wait_ge(k0_lo, 2 * TILES + CREDIT)
            pe.wait_ge(v0_kept, TILES)
            pe.wait_ge(y0_cols, CREDIT + TILES)
            for b in range(LAYERS):
                queries(b, 0, first_q[b])
                pe.wait_ge(side_done, first_q[b] + 1)
                score(b, 0, 0)
                score(b, 0, 1)
                for g in range(BLOCKS):
                    if b and g == 2:
                        feed(0, TILES - 1, last_f0)
                    if b and g == 6:
                        keys(last_f0 + 1)
                    if b and g == 10:
                        values(last_f0 + 2)
                    if g == 15:
                        queries(b, 1, 1 if b == 0 else last_f0 + 3)
                    if g + 2 < BLOCKS:
                        if b and g + 2 == BLOCKS - BPT:
                            pe.wait_ge(side_done, last_f0 + 3)
                        score(b, 0, g + 2)
                    if g == 0:
                        pe.wait_ge(att_kept, CREDIT + TILES * b)
                    weigh(b, 0, g)
                with pe.Fori(1, TILES) as t:
                    f = job_f(b, t - 1)
                    pe.wait_ge(side_done, f)
                    score(b, t, 0)
                    score(b, t, 1)
                    for g in range(BLOCKS):
                        if g == 2:
                            feed(b, t - 1, f)
                        if g == 6 and b == 0:
                            keys(f + 1)
                        if g == 6 and b == 1:
                            y_to_rows(f + 1)
                        if g == 10 and b == 0:
                            values(f + 2)
                        if g == 15:
                            queries(b, t + 1, f + (3 if b == 0 else 2))
                        if g + 2 < BLOCKS:
                            score(b, t, g + 2)
                        if g == 0:
                            pe.wait_ge(att_kept, CREDIT + TILES * b + t)
                        weigh(b, t, g)
            feed(1, TILES - 1, job_f(1, TILES - 1))
            y_to_rows(job_f(1, TILES - 1) + 1)

            pe.wait_ge(tanh_done, SLOTS + LAYERS * TILES * BLOCKS)
            for t in range(TILES):
                pe.wait_ge(unit_staged, t + 1)
                turn(bank(t), (relu_stage, exp_stage)[t % 2]).then_inc(unit_turned, 1)
            pe.wait_ge(unit_lo_kept, TILES)
            with pe.Fori(0, TILES) as q:
                for i in range(BPT):
                    pe.wait_ge(block_staged, BPT * q + i + 1)
                    hi, lo = block_split[i % 2][:, 0:P], block_split[i % 2][:, P:2 * P]
                    for n in range(TILES):
                        u = TILES * i + n
                        pe.wait_ge(cos_kept, BPT * TILES * q + u + 1)
                        nodes = slice(n * TW, (n + 1) * TW)
                        dst = bank(u % BANKS)
                        pe.matmul(dst, hi, unit_hi[:, nodes], start=True, stop=False)
                        pe.matmul(dst, hi, unit_lo[:, nodes], start=False, stop=False)
                        pe.matmul(dst, lo, unit_hi[:, nodes], start=False, stop=True).then_inc(cos_ready, 1)

            pe.wait_ge(cos_kept, BANKS + BLOCKS * TILES)

            def w_cheb(b, k):
                return cheb_s[:, (b * 3 + k) * P:(b * 3 + k + 1) * P]

            def turn_a(b, tau):
                pe.wait_ge(a_staged, TILES * b + tau + 1)
                pe.wait_ge(a_lo_kept, CREDIT + TILES * b + tau)
                turn(bank(6), sum_stage).then_inc(a_turned, 1)

            def mix_h(b, tau):
                pe.wait_ge(h_staged, CREDIT + TILES * b + tau)
                pe.matmul(bank(7), w_cheb(b, 0), plane_y[:, tile(tau)], start=True, stop=False)
                pe.matmul(bank(7), w_cheb(b, 1), a_cols[:, tile(tau)], start=False, stop=False)
                pe.wait_ge(t2_kept, TILES * b + tau + 1)
                pe.matmul(bank(7), w_cheb(b, 2), y_stage[:, :], start=False, stop=True).then_inc(mix_ready, 1)

            def turn_h(b, tau):
                pe.wait_ge(h_staged, CREDIT + TILES * b + tau + 1)
                pe.wait_ge(h_lo_kept, CREDIT + TILES * b + tau)
                turn(bank(6), turn_stage).then_inc(h_turned, 1)

            def chunk_steps(n_pass, t, c, what, b, tau, *z):
                if what == "a" and c == 2:
                    turn_a(b, tau)
                if what == "h" and c == 2:
                    mix_h(b, tau)
                if what == "h" and c == 7:
                    turn_h(b, tau)
                if n_pass == 1 and c == 8:
                    pe.wait_ge(x1_staged, t + 1)
                    pe.wait_ge(x1_cols, CREDIT + t)
                    turn(bank(7), turn_stage).then_inc(x1_turned, 1)
                adj_chunk(n_pass, t, c, *z)

            for n_pass in range(1, 1 + 2 * LAYERS):
                b, half = (n_pass - 1) // 2, (n_pass - 1) % 2
                z = (a_hi, a_lo, hi_cheb, lo_cheb) if half else (z_hi, z_lo, hi_cheb, lo_cheb)
                for c in range(CHUNKS):
                    if c % (BPT // CH) == 0:
                        z_tile = c // (BPT // CH)
                        if half:
                            pe.wait_ge(a_lo_kept, CREDIT + TILES * b + z_tile + 1)
                        elif b:
                            pe.wait_ge(h_lo_kept, CREDIT + z_tile + 1)
                        else:
                            pe.wait_ge(x1_lo, z_tile + 1)
                    what = ("a", b, TILES - 1) if half else ("h" if b else "", b - 1, TILES - 1)
                    chunk_steps(n_pass, 0, c, *what, *z)
                with pe.Fori(1, TILES) as t:
                    for c in range(CHUNKS):
                        chunk_steps(n_pass, t, c, "ah"[half], b, t - 1, *z)
            mix_h(LAYERS - 1, TILES - 1)
            turn_h(LAYERS - 1, TILES - 1)

        @block.vector
        def _(dve):
            def copy(dst, src):
                return dve.tensor_scalar(dst, src, 1.0, None, ALU.mult)

            def sub(dst, a, b):
                return dve.tensor_tensor(out=dst, in0=a, in1=b.bitcast(F32), op=ALU.subtract)

            def low_part(n_pass, t, c, his, los):
                dve.wait_ge(hi_kept, chunk_no(n_pass, t, c) + 1)
                sub(los[c % SPLITS][:, :], raw_slots(n_pass)[c % RAWS][:, :], his[c % SPLITS][:, :]).then_inc(lo_kept, 1)

            for g in range(TILES):
                dve.wait_ge(h0_split, g + 1)
                sub(h0_lo[:, g * TW:(g + 1) * TW], bank(g), h0_hi[:, g * TW:(g + 1) * TW])
                copy(xh[:, g * BPT:(g + 1) * BPT, P:2 * P], cols(bank(g))).then_inc(h0_kept, 1)
            for i in range(BLOCKS // 2):
                dve.wait_ge(uc_ready, i + 1)
                if i:
                    dve.wait_ge(uc_summed, i)
                prod = cols(exp_stage[:, 0:2 * P])
                dve.tensor_tensor(out=prod, in0=cols(bank(i % 6), 2 * P)[:, :, 0:P], in1=xh[:, 2 * i:2 * i + 2, 0:P],
                                  op=ALU.mult).then_inc(uc_squared, 1)
                dve.wait_ge(uc_squared, i + 1)
                dve.tensor_reduce(squares[:, 2 * i:2 * i + 2], prod, AX_X, ALU.add).then_inc(uc_summed, 1)

            def agg_of(tau):
                dve.wait_ge(gate_ready, 2 * tau + CREDIT)
                dve.wait_ge(chunk_used, tile_done(0, tau))
                dve.tensor_tensor(out=sum_stage[:, :], in0=ps[:, tile(tau)], in1=plane_y[:, tile(tau)],
                                  op=ALU.add).then_inc(agg_kept, 1)

            def gate_of(tau):
                dve.wait_ge(gate_ready, 2 * tau + CREDIT + 2)
                dve.wait_ge(gate_relu, tau + 1)
                dve.tensor_tensor(out=relu_stage[:, :], in0=bank(7), in1=relu_stage[:, :], op=ALU.mult).then_inc(
                    gated, 1)

            def y0_of(tau):
                dve.wait_ge(h2_ready, tau + 1)
                dve.wait_ge(gated, tau + 1)
                dve.wait_ge(kv_ready, 2 * tau + CREDIT)
                dve.wait_ge(y0_cols, CREDIT + tau)
                dve.tensor_tensor(out=y_stage[:, :], in0=ps[:, tile(tau)], in1=relu_stage[:, :], op=ALU.add).then_inc(
                    y0_kept, 1)

            def k0_lo_of(tau):
                for h in range(HEADS):
                    dve.wait_ge(k0_hi, 2 * tau + h + 1)
                    k = k_split[0][h]
                    sub(k[DH:P, tile(tau)], bank(7)[h * DH:(h + 1) * DH, :], k[0:DH, tile(tau)]).then_inc(k0_lo, 1)

            for c in range(CHUNKS):
                low_part(0, 0, c, hi_front, lo_front)
                if c == 3:
                    dve.wait_ge(norm_kept, 1)
                    dve.wait_ge(uc_kept, BLOCKS // 2)
                if c in (3, 4, 5):
                    for t in (2 * (c - 3), 2 * (c - 3) + 1):
                        part = xh[:, BPT * t:BPT * (t + 1), P:2 * P]
                        scale = inv_norm[:, BPT * t:BPT * (t + 1)].unsqueeze(2).to_broadcast([P, BPT, P])
                        dve.tensor_tensor(out=part, in0=part, in1=scale, op=ALU.mult).then_inc(corr_scaled, 1)
            dve.wait_ge(corr_kept, TILES)
            with dve.Fori(1, TILES) as t:
                for c in range(CHUNKS):
                    low_part(0, t, c, hi_front, lo_front)
                    if c == 3:
                        agg_of(t - 1)
                    if c == 6:
                        gate_of(t - 1)
                    if c == 9:
                        y0_of(t - 1)
                    if c == 11:
                        k0_lo_of(t - 1)
            agg_of(TILES - 1)
            gate_of(TILES - 1)
            y0_of(TILES - 1)
            k0_lo_of(TILES - 1)

            def att_of(b, tau):
                dve.wait_ge(probs_used, SLOTS + BLOCKS * (TILES * b + 1) + tau * BLOCKS)
                copy(sum_stage[:, :], bank(6)).then_inc(att_kept, 1)

            def y_of(b, tau):
                dve.wait_ge(relu_kept, TILES * b + tau + 1)
                dve.tensor_tensor(out=y_stage[:, :], in0=plane_y[:, tile(tau)], in1=relu_stage[:, :],
                                  op=ALU.add).then_inc(side_done, 1)

            def k_lo_of(tau):
                for h in range(HEADS):
                    dve.wait_ge(k_hi_kept, 2 * tau + h + 1)
                    k = k_split[1][h]
                    ins = sub(k[DH:P, tile(tau)], bank(7)[h * DH:(h + 1) * DH, :], k[0:DH, tile(tau)])
                ins.then_inc(side_done, 1)

            def v_of(tau, job):
                dve.wait_ge(side_ready, job + 1)
                copy(v_rows[1][:, tile(tau)], bank(7)).then_inc(side_done, 1)

            def q_lo_of(t, n):
                for h in range(HEADS):
                    dve.wait_ge(q_hi_kept, 4 * n + 2 * h + 2)
                    for z in range(2):
                        part = slice(z * DH, (z + 1) * DH)
                        ins = sub(q_lo[h][part, tile(t)], bank(7)[h * DH:(h + 1) * DH, :], q_hi[h][part, tile(t)])
                ins.then_inc(side_done, 1)

            def rows_of(tau, job):
                dve.wait_ge(side_ready, job + 1)
                copy(y_rows[:, tile(tau)], bank(7)).then_inc(side_done, 1)
                dve.wait_ge(side_done, job + 1)
                dve.tensor_tensor(out=exp_stage[:, :], in0=y_rows[:, tile(tau)], in1=y_rows[:, tile(tau)],
                                  op=ALU.mult).then_inc(y_squared, 1)
                dve.wait_ge(y_squared, 2 * tau + 1)
                dve.tensor_reduce(squares[:, bass.ds(BPT * tau, BPT)], cols(exp_stage[:, :]), AX_X,
                                  ALU.add).then_inc(y_squared, 1)

            for b in range(LAYERS):
                q_lo_of(0, 7 * b)
                if b:
                    att_of(0, TILES - 1)
                    y_of(0, TILES - 1)
                    dve.wait_ge(side_done, last_f0 + 1)
                    copy(plane_y[:, (TILES - 1) * TW:N], y_stage[:, :])
                    k_lo_of(TILES - 1)
                    v_of(TILES - 1, last_f0 + 2)
                q_lo_of(1, 7 * b + 1)
                with dve.Fori(1, TILES) as t:
                    f = job_f(b, t - 1)
                    att_of(b, t - 1)
                    y_of(b, t - 1)
                    if b == 0:
                        dve.wait_ge(side_done, f + 1)
                        copy(plane_y[:, tile(t, -1)], y_stage[:, :])
                        k_lo_of(t - 1)
                        v_of(t - 1, f + 2)
                    else:
                        rows_of(t - 1, f + 1)
                    q_lo_of(t + 1, 7 * b + t + 1)
            f = job_f(1, TILES - 1)
            att_of(1, TILES - 1)
            y_of(1, TILES - 1)
            rows_of(TILES - 1, f + 1)

            dve.wait_ge(y_squared, 2 * TILES)
            dve.tensor_scalar(squares[:, :], squares[:, :], P * 1e-6, None, ALU.add).then_inc(sum_eps, 1)
            dve.wait_ge(fl_kept, 1)

            def unit_lo_of(t):
                dve.wait_ge(unit_hi_kept, t + 1)
                nodes = slice(t * TW, (t + 1) * TW)
                sub(unit_lo[:, nodes], bank(t), unit_hi[:, nodes]).then_inc(unit_lo_kept, 1)

            for t in range(TILES):
                if t >= 2:
                    dve.wait_ge(unit_turned, t - 1)
                scale = inv_norm[:, BPT * t:BPT * (t + 1)].unsqueeze(2).to_broadcast([P, BPT, P])
                dve.tensor_tensor(out=cols((relu_stage, exp_stage)[t % 2][:, :]), in0=cols(y_rows[:, t * TW:(t + 1) * TW]),
                                  in1=scale, op=ALU.mult).then_inc(unit_staged, 1)
                if t:
                    unit_lo_of(t - 1)
            unit_lo_of(TILES - 1)

            def per_block(ap, q, n):
                return ap[:, BPT * q:BPT * (q + 1)].unsqueeze(2).to_broadcast([P, BPT, n])

            def of_tile(ap, q):
                return cols(ap[:, :], TOP)[:, BPT * q:BPT * (q + 1), :]

            steps = 0

            def shares(q):
                nonlocal steps
                dve.wait_ge(exp_done, 2 + BPT * (q + 1))
                r = exp_sum[:, BPT * q:BPT * (q + 1)]
                dve.reciprocal(r, r).then_inc(weight_step, 1)
                dve.wait_ge(weight_step, steps + 1)
                dve.wait_ge(weight_exp, 2 * q + 1)
                dve.tensor_tensor(out=of_tile(weight_p, q), in0=of_tile(weight_e, q), in1=per_block(exp_sum, q, TOP),
                                  op=ALU.mult).then_inc(weight_step, 1)
                dve.wait_ge(weight_step, steps + 2)
                steps += 2
                first = of_tile(weight_p, q)[:, :, 0:1].to_broadcast([P, BPT, TOP])
                dve.tensor_tensor(out=of_tile(weight_e, q), in0=of_tile(weight_p, q), in1=first,
                                  op=ALU.subtract).then_inc(weight_diff, 1)

            def weights(q):
                nonlocal steps
                dve.wait_ge(weight_exp, 2 * q + 2)
                r = exp_sum[:, BPT * q:BPT * (q + 1)]
                dve.tensor_reduce(r, of_tile(weight_e, q), AX_X, ALU.add).then_inc(weight_step, 1)
                dve.wait_ge(weight_step, steps + 1)
                dve.reciprocal(r, r).then_inc(weight_step, 1)
                dve.wait_ge(weight_step, steps + 2)
                steps += 2
                dve.tensor_tensor(out=of_tile(weight, q), in0=of_tile(weight_e, q), in1=per_block(exp_sum, q, TOP),
                                  op=ALU.mult).then_inc(weight_kept, 1)

            ln_steps = 2 * BPT

            def variances(src, before):
                for i in range(BPT):
                    dve.bn_stats(stats[:, 6 * i:6 * i + 6], src[:, i * P:(i + 1) * P]).then_inc(ln_step, 1)
                dve.wait_ge(ln_step, before + BPT)
                dve.memset(var_eps[:, :], 1e-5)
                for i in range(BPT):
                    dve.bn_aggr(mean_var[:, 2 * i:2 * i + 2], stats[:, 6 * i:6 * i + 6]).then_inc(ln_step, 1)
                dve.wait_ge(ln_step, before + ln_steps)
                dve.tensor_tensor(out=var_eps[:, :], in0=var_eps[:, :], in1=cols(mean_var[:, :], 2)[:, :, 1],
                                  op=ALU.add).then_inc(ln_var, 1)

            def normal(dst, src, i):
                return dve.tensor_scalar(dst[:, i * P:(i + 1) * P], src[:, i * P:(i + 1) * P],
                                         mean_var[:, 2 * i:2 * i + 1], inv_std[:, i:i + 1], ALU.subtract, ALU.mult)

            for j in range(BLOCKS + 9):
                if j < BLOCKS:
                    dve.wait_ge(cos_kept, BANKS + TILES * (j + 1))
                    top = top_v[:, j * 8:(j + 1) * 8]
                    dve.max(top, cos_rows[j % 2][:, :]).then_inc(top_done, 1)
                    dve.wait_ge(top_done, j + 1)
                    dve.max_index(top_i[:, j * 8:(j + 1) * 8], top, cos_rows[j % 2][:, :]).then_inc(index_done, 1)
                if (j - 5) % BPT == 0 and 0 <= (j - 5) // BPT < TILES:
                    shares((j - 5) // BPT)
                if (j - 8) % BPT == 0 and 0 <= (j - 8) // BPT < TILES:
                    weights((j - 8) // BPT)
                if (j - 10) % BPT == 0 and 0 <= (j - 10) // BPT < TILES:
                    q = (j - 10) // BPT
                    dve.wait_ge(mixed, BPT * (q + 1))
                    variances(plane_x[:, q * TW:(q + 1) * TW], q * ln_steps)
                if (j - 12) % BPT == 0 and 0 <= (j - 12) // BPT < TILES:
                    q = (j - 12) // BPT
                    nodes = slice(q * TW, (q + 1) * TW)
                    dve.wait_ge(ln_power, q + 1)
                    for i in range(BPT):
                        ins = normal(plane_x[:, nodes], plane_x[:, nodes], i)
                    ins.then_inc(x1_kept, 1)
                    dve.wait_ge(x1_kept, q + 1)
                    copy(z_hi[:, nodes], plane_x[:, nodes]).then_inc(x1_hi, 1)
                    dve.wait_ge(x1_hi, q + 1)
                    sub(z_lo[:, nodes], plane_x[:, nodes], z_hi[:, nodes]).then_inc(x1_lo, 1)

            def a_cols_of(b, tau):
                dve.wait_ge(a_staged, TILES * b + tau + 1)
                copy(a_cols[:, tile(tau)], sum_stage[:, :]).then_inc(a_cols_kept, 1)

            def a_lo_of(b, tau):
                dve.wait_ge(a_hi_kept, TILES * b + tau + 1)
                sub(a_lo[:, tile(tau)], bank(6), a_hi[:, tile(tau)]).then_inc(a_lo_kept, 1)

            def t2_of(b, tau):
                dve.wait_ge(chunk_used, tile_done(2 + 2 * b, tau))
                dve.wait_ge(mix_ready, CREDIT + TILES * b + tau)
                dve.scalar_tensor_tensor(out=y_stage[:, :], in0=ps[:, tile(tau)], scalar=2.0, in1=plane_y[:, tile(tau)],
                                         op0=ALU.mult, op1=ALU.subtract).then_inc(t2_kept, 1)

            def neg_of(b, tau):
                dve.wait_ge(pos_kept, TILES * b + tau + 1)
                dve.tensor_scalar(exp_stage[:, :], bank(7), chebb_s[:, b:b + 1], 0.0, ALU.add, ALU.min).then_inc(
                    neg_kept, 1)

            def h_of(b, tau):
                dve.wait_ge(exp_kept, TILES * b + tau + 1)
                dve.wait_ge(h_turned, CREDIT + TILES * b + tau)
                dve.scalar_tensor_tensor(out=turn_stage[:, :], in0=exp_stage[:, :], scalar=-1.0, in1=relu_stage[:, :],
                                         op0=ALU.add, op1=ALU.add).then_inc(h_staged, 1)
                if b == 0:
                    dve.wait_ge(h_staged, CREDIT + tau + 1)
                    copy(plane_y[:, tile(tau)], turn_stage[:, :])

            def h_lo_of(tau):
                dve.wait_ge(h_hi_kept, tau + 1)
                sub(z_lo[:, tile(tau)], bank(6), z_hi[:, tile(tau)]).then_inc(h_lo_kept, 1)

            def result_sum(tau):
                dve.wait_ge(h_turned, CREDIT + TILES * (LAYERS - 1) + tau + 1)
                dve.tensor_tensor(out=sum_stage[:, :], in0=bank(6), in1=plane_x[:, tile(tau)], op=ALU.add).then_inc(
                    h_lo_kept, 1)
                dve.wait_ge(h_lo_kept, CREDIT + TILES * (LAYERS - 1) + tau + 1)
                variances(sum_stage, TILES * ln_steps + tau * ln_steps)

            def result(tau):
                dve.wait_ge(ln_power, TILES + 1 + tau)
                dve.wait_ge(out_free, CREDIT + tau)
                for i in range(BPT):
                    ins = normal(out_stage, sum_stage, i)
                ins.then_inc(row_out, 1)

            def chunk_steps(n_pass, t, c, what, b, tau):
                low_part(n_pass, t, c, hi_cheb, lo_cheb)
                if what == "a" and c == 4:
                    a_cols_of(b, tau)
                if what == "a" and c == 6:
                    a_lo_of(b, tau)
                if what == "h" and c == 3:
                    t2_of(b, tau)
                if what == "h" and c == 6:
                    neg_of(b, tau)
                if what == "h" and c == 7:
                    h_of(b, tau)
                if what == "h" and c == 10:
                    if b == 0:
                        h_lo_of(tau)
                    else:
                        result_sum(tau)
                if what == "h" and c == 11 and b:
                    result(tau)

            for n_pass in range(1, 1 + 2 * LAYERS):
                b, half = (n_pass - 1) // 2, (n_pass - 1) % 2
                for c in range(CHUNKS):
                    if half:
                        chunk_steps(n_pass, 0, c, "a", b, TILES - 1)
                    else:
                        chunk_steps(n_pass, 0, c, "h" if b else "", b - 1, TILES - 1)
                with dve.Fori(1, TILES) as t:
                    for c in range(CHUNKS):
                        chunk_steps(n_pass, t, c, "ah"[half], b, t - 1)
            t2_of(LAYERS - 1, TILES - 1)
            neg_of(LAYERS - 1, TILES - 1)
            h_of(LAYERS - 1, TILES - 1)
            result_sum(TILES - 1)
            result(TILES - 1)


def kernel(x, adj, L0_gnn_w_h, L0_gnn_w_hf, L0_gnn_wq, L0_gnn_wk, L0_gnn_wv, L0_gnn_ffn_w, L0_gnn_ffn_b,
           L1_gnn_W0, L1_gnn_b0, L1_gnn_W1, L1_gnn_b1):
    import numpy as np
    import concourse.bacc as bacc
    from concourse.bass_utils import run_bass_kernel_spmd

    def rows(a):
        a = np.asarray(a)
        return a.reshape(-1, P, a.shape[-1]).transpose(1, 0, 2).reshape(P, -1)

    def side(w):
        return np.asarray(w).transpose(2, 0, 1).reshape(P, -1)

    adj_t = np.asarray(adj).reshape(TILES, TW, BLOCKS, P).transpose(3, 0, 2, 1).reshape(P, -1)
    cheb = np.concatenate([np.asarray(L1_gnn_W0), np.asarray(L1_gnn_W1)], axis=0)
    arrays = {
        "x_rows": rows(x),
        "x_cols": np.asarray(x).T,
        "adj_t": adj_t,
        "w_h": np.asarray(L0_gnn_w_h).T,
        "w_hf": np.asarray(L0_gnn_w_hf).T,
        "wq": side(L0_gnn_wq),
        "wk": side(L0_gnn_wk),
        "wv": side(L0_gnn_wv),
        "ffn_w": side(L0_gnn_ffn_w),
        "ffn_b": np.asarray(L0_gnn_ffn_b).T,
        "cheb_w": cheb.transpose(1, 0, 2).reshape(P, -1),
        "cheb_b": np.stack([np.asarray(L1_gnn_b0), np.asarray(L1_gnn_b1)], axis=1),
    }
    arrays = {k: np.ascontiguousarray(v) for k, v in arrays.items()}
    nc = bacc.Bacc("TRN2", target_bir_lowering=False, num_devices=1)
    args = [nc.dram_tensor(f"in_{k}", v.shape, F32, kind="ExternalInput").ap() for k, v in arrays.items()]
    out = nc.dram_tensor("out_rows", (P, N), F32, kind="ExternalOutput").ap()
    gnn_kernel(nc, *args, out)
    r = run_bass_kernel_spmd(nc, [{f"in_{k}": v for k, v in arrays.items()}], core_ids=[0])
    got = r.results[0]["out_rows"]
    return np.ascontiguousarray(got.reshape(P, BLOCKS, P).transpose(1, 0, 2).reshape(N, P))
```

```python
from contextlib import ExitStack

import concourse.bass as bass
from concourse import mybir

P = 128
F32 = mybir.dt.float32
F32R = mybir.dt.float32r
BF16 = mybir.dt.bfloat16
U32 = mybir.dt.uint32
ALU = mybir.AluOpType
ACT = mybir.ActivationFunctionType
AX_X = mybir.AxisListType.X

N = 3072
TW = 512
TILES = N // TW
BLOCKS = N // P
BPT = TW // P
CH = 2
CW = CH * TW
CHUNKS = BLOCKS // CH
RAWS = 6
SPLITS = 4
HEADS = 2
DH = P // HEADS
LAYERS = 2
SLOTS = 3
BANKS = 8
TOP = 3
GATHERS = 10
POOL_X1 = range(3)
POOL_MIXES = 18
UC_BANKS = 5
CREDIT = 1
KB = 1024


def tile(t, shift=0):
    return bass.ds((t + shift) * TW, TW)


def cols(ap, n=P):
    return ap.rearrange("p (j k) -> p j k", k=n)


def gnn_kernel(nc, x_rows_d, x_cols_d, adj_t, w_h, w_hf, wq, wk, wv, ffn_w, ffn_b, cheb_w, cheb_b, out):
    with ExitStack() as ctx:
        def sb(name, width, dt=F32):
            return ctx.enter_context(nc.sbuf_tensor(name, [P, width], dt))

        def sem(name):
            return ctx.enter_context(nc.semaphore(name))

        def sems(name, n):
            return [sem(f"{name}{i}") for i in range(n)]

        ps = ctx.enter_context(nc.psum_tensor("ps", [P, BANKS * TW], F32))

        def bank(k):
            return ps[:, k * TW:(k + 1) * TW]

        plane_x = sb("plane_x", N)
        plane_y = sb("plane_y", N)
        wh_s = sb("wh_s", 3 * P)
        whf_s = sb("whf_s", 2 * P)
        wq_s = sb("wq_s", LAYERS * P)
        wk_s = sb("wk_s", LAYERS * P)
        wv_s = sb("wv_s", LAYERS * P)
        ffn_s = sb("ffn_s", LAYERS * P)
        ffnb_s = sb("ffnb_s", LAYERS)
        cheb_s = sb("cheb_s", LAYERS * 3 * P)
        chebb_s = sb("chebb_s", LAYERS)
        ident = sb("ident", P)
        gram = sb("gram", 2 * P)
        cheb_mix = sb("cheb_mix", LAYERS * 2 * P)
        half_power = sb("half_power", 1)
        sum_stage = sb("sum_stage", TW)
        y_stage = sb("y_stage", TW)
        relu_stage = sb("relu_stage", TW)
        exp_stage = sb("exp_stage", TW)
        turn_stage = sb("turn_stage", TW)
        out_stage = sb("out_stage", TW)
        block_split = [sb(f"block_split{i}", 2 * P, F32R) for i in range(2)]
        top_v = sb("top_v", BLOCKS * 8)
        top_i = sb("top_i", BLOCKS * 8, U32)
        squares = sb("squares", BLOCKS)
        inv_norm = sb("inv_norm", BLOCKS)
        exp_sum = sb("exp_sum", BLOCKS)
        weight_e = sb("weight_e", BLOCKS * TOP)
        weight_p = sb("weight_p", BLOCKS * TOP)
        weight = sb("weight", BLOCKS * TOP)
        stats = sb("stats", BPT * 6)
        mean_var = sb("mean_var", BPT * 2)
        var_eps = sb("var_eps", BPT)
        inv_std = sb("inv_std", BPT)

        base = -(-nc.sbuf_base // 32) * 32

        def at(name, kb, width, dt=F32):
            return nc.alloc_sbuf_tensor_at(name, [P, width], dt, offset=base + kb * KB)

        k_split = [[at(f"k_split{b}{h}", 36 * b + 12 * h, N, F32R) for h in range(HEADS)] for b in range(LAYERS)]
        v_rows = [at(f"v_rows{b}", 36 * b + 24, N) for b in range(LAYERS)]
        xh = cols(at("xh", 36, 2 * N)[:, :], 2 * P)
        raws_front = [at(f"raw_front{i}", 60 + 4 * i, CW) for i in range(RAWS)]
        hi_front = [at(f"hi_front{i}", 84 + 4 * i, CW, F32R) for i in range(SPLITS)]
        lo_front = [at(f"lo_front{i}", 100 + 4 * i, CW, F32R) for i in range(SPLITS)]
        h0_hi, h0_lo = at("h0_hi", 116, N, F32R), at("h0_lo", 128, N, F32R)
        q_hi = [at(f"q_hi{h}", 72 + 24 * h, N, F32R) for h in range(HEADS)]
        q_lo = [at(f"q_lo{h}", 84 + 24 * h, N, F32R) for h in range(HEADS)]
        probs_all = at("probs", 128, SLOTS * HEADS * TW)
        probs = [probs_all[:, s * HEADS * TW:(s + 1) * HEADS * TW] for s in range(SLOTS)]
        y_rows = at("y_rows", 0, N)
        unit_hi, unit_lo = at("unit_hi", 12, N, F32R), at("unit_lo", 24, N, F32R)
        cos_rows = [at(f"cos_rows{i}", 36 + 12 * i, N) for i in range(2)]
        gather = cols(at("gather", 60, GATHERS * TOP * P)[:, :])
        exp_dump = at("exp_dump", 75, N, BF16)
        adj_kept = at("adj_kept", 81, TILES * CW)
        z_hi, z_lo = at("z_hi", 113, N, F32R), at("z_lo", 125, N, F32R)
        raws_cheb = [at(f"raw_cheb{i}", (0 if i < 3 else 125) + 4 * i, CW) for i in range(RAWS)]
        a_cols = at("a_cols", 12, N)
        a_hi, a_lo = at("a_hi", 24, N, F32R), at("a_lo", 60, N, F32R)
        hi_cheb = [at(f"hi_cheb{i}", 36 + 4 * i, CW, F32R) for i in range(SPLITS)]
        lo_cheb = [at(f"lo_cheb{i}", (52 if i < 2 else 97) + 4 * i, CW, F32R) for i in range(SPLITS)]
        assert base + 149 * KB <= nc.sbuf_usable_end

        y_dram = nc.dram_tensor("y_scratch", [N, P], F32)

        loaded_first, loaded, x_in = sem("loaded_first"), sem("loaded"), sems("x_in", TILES)
        rows_in, consts_set, ident_set = sem("rows_in"), sem("consts_set"), sem("ident_set")
        adj_in, kept_in = sems("adj_in", RAWS), sem("kept_in")
        hi_kept, lo_kept, chunk_used = sem("hi_kept"), sem("lo_kept"), sem("chunk_used")
        h0_ready, h0_split, h0_kept = sem("h0_ready"), sem("h0_split"), sem("h0_kept")
        gram_ready, gram_kept = sem("gram_ready"), sem("gram_kept")
        uc_ready, uc_squared, uc_summed, uc_kept = sem("uc_ready"), sem("uc_squared"), sem("uc_summed"), sem("uc_kept")
        norm_kept, corr_scaled, corr_turned, corr_kept = (
            sem("norm_kept"), sem("corr_scaled"), sem("corr_turned"), sem("corr_kept"))
        agg_kept, gate_ready, gate_relu, gated = sem("agg_kept"), sem("gate_ready"), sem("gate_relu"), sem("gated")
        h2_ready, y0_kept, y0_cols = sem("h2_ready"), sem("y0_kept"), sem("y0_cols")
        kv_ready, k0_hi, k0_lo, v0_kept = sem("kv_ready"), sem("k0_hi"), sem("k0_lo"), sem("v0_kept")
        scores_ready, tanh_done, probs_used = sem("scores_ready"), sem("tanh_done"), sem("probs_used")
        att_kept = sem("att_kept")
        side_ready, side_done = sem("side_ready"), sem("side_done")
        relu_kept, k_hi_kept, q_hi_kept = sem("relu_kept"), sem("k_hi_kept"), sem("q_hi_kept")
        y_squared = sem("y_squared")
        y_out, x_again = sem("y_out"), sem("x_again")
        fl_kept, unit_staged, unit_hi_kept = sem("fl_kept"), sem("unit_staged"), sem("unit_hi_kept")
        block_staged, cos_ready, cos_kept = sem("block_staged"), sem("cos_ready"), sem("cos_kept")
        exp_done, top_done, index_done = sem("exp_done"), sem("top_done"), sem("index_done")
        gathered = sems("gathered", BLOCKS)
        weight_exp, weight_diff, weight_step, weight_kept = (
            sem("weight_exp"), sem("weight_diff"), sem("weight_step"), sem("weight_kept"))
        mix_step, mixed, mix_last_step = sem("mix_step"), sem("mixed"), sem("mix_last_step")
        ln_step, ln_var, ln_power = sem("ln_step"), sem("ln_var"), sem("ln_power")
        x1_kept, x1_hi, x1_lo = sem("x1_kept"), sem("x1_hi"), sem("x1_lo")
        x1_staged, x1_turned, x1_cols = sem("x1_staged"), sem("x1_turned"), sem("x1_cols")
        a_staged, a_turned, a_cols_kept = sem("a_staged"), sem("a_turned"), sem("a_cols_kept")
        a_hi_kept, a_lo_kept = sem("a_hi_kept"), sem("a_lo_kept")
        weights_mixed, pos_kept, neg_kept, exp_kept = (
            sem("weights_mixed"), sem("pos_kept"), sem("neg_kept"), sem("exp_kept"))
        h_staged, h_turned, h_hi_kept, h_lo_kept = sem("h_staged"), sem("h_turned"), sem("h_hi_kept"), sem("h_lo_kept")
        row_out, stored = sem("row_out"), sem("stored")

        start_values = {
            lo_kept: RAWS, chunk_used: SPLITS,
            tanh_done: SLOTS, probs_used: SLOTS, cos_kept: BANKS, index_done: 2, exp_done: 2,
            gate_ready: CREDIT, k0_lo: CREDIT, kv_ready: CREDIT, y0_kept: CREDIT, y0_cols: CREDIT, att_kept: CREDIT,
            x1_turned: CREDIT, x1_cols: CREDIT, a_turned: CREDIT, a_cols_kept: CREDIT, a_lo_kept: CREDIT,
            h_staged: CREDIT, h_turned: CREDIT, h_lo_kept: CREDIT, row_out: CREDIT,
        }

        first_q, last_tile, second_q = [0, 26], [1, 27], [6, 30]

        def job_f(b, tau):
            return [7, 31][b] + 4 * tau

        last_f = job_f(1, TILES - 1) - 1
        last_side = last_f + 3

        block = ctx.enter_context(nc.Block())

        def chunk_no(n_pass, t, c):
            return CHUNKS * TILES * n_pass + c + t * CHUNKS

        def uc_bank(i):
            return 1 + i % UC_BANKS

        def split_no(n_pass, t, c):
            whole = n_pass > 1 or (n_pass == 1 and not (isinstance(t, int) and t == 0))
            return chunk_no(n_pass, t, c) - (CHUNKS if whole else 0)

        def tile_done(n_pass, tau):
            return SPLITS + CHUNKS * (TILES * n_pass + 1) + tau * CHUNKS

        def is_kept(n_pass, c):
            return n_pass > 0 and c == CHUNKS - 1

        def raw_chunk(n_pass, t, c):
            if is_kept(n_pass, c):
                return adj_kept[:, bass.ds(t * CW, CW)]
            return (raws_front if n_pass == 0 else raws_cheb)[c % RAWS][:, :]

        def loads_before(n_pass, c):
            per_tile = CHUNKS // RAWS
            before = per_tile * TILES * n_pass
            if n_pass > 0 and c % RAWS == (CHUNKS - 1) % RAWS:
                before -= TILES * (n_pass - 1)
                per_tile -= 1
            return before, per_tile

        def wait_chunk(engine, n_pass, t, c):
            before, per_tile = loads_before(n_pass, c)
            if not is_kept(n_pass, c):
                engine.wait_ge(adj_in[c % RAWS], 16 * (before + c // RAWS + 1) + t * (16 * per_tile))
            elif n_pass == 1:
                engine.wait_ge(kept_in, 16 + t * 16)

        @block.sync
        def _(sp):
            def fetch(n_pass, t, c, signal):
                sp.dma_start(raw_chunk(n_pass, t, c), adj_t[:, bass.ds(t * (BLOCKS * TW) + c * CW, CW)]).then_inc(
                    signal, 16)

            def load(n_pass, t, c):
                if n_pass == 1 and isinstance(t, int) and RAWS <= t * CHUNKS + c < RAWS + CHUNKS:
                    sp.wait_ge(chunk_used, SPLITS + chunk_no(n_pass, t, c) - RAWS + 1)
                else:
                    sp.wait_ge(lo_kept, split_no(n_pass, t, c) + 1)
                fetch(n_pass, t, c, adj_in[c % RAWS])

            sp.dma_start(wh_s[:, :], w_h).then_inc(loaded_first, 16)
            for t in range(TILES):
                sp.dma_start(plane_x[:, t * TW:(t + 1) * TW], x_cols_d[:, t * TW:(t + 1) * TW]).then_inc(x_in[t], 16)
            sp.dma_start(xh[:, :, 0:P], cols(x_rows_d)).then_inc(rows_in, 16)
            for n_pass in range(1 + 2 * LAYERS):
                if n_pass == 1:
                    with sp.Fori(0, TILES) as t:
                        sp.wait_ge(side_done, job_f(1, 0) + 2 + t * 4)
                        sp.dma_start(y_dram[:, :].rearrange("(j p) d -> p j d", p=P)[:, bass.ds(t * BPT, BPT), :],
                                     cols(y_rows[:, tile(t)])).then_inc(y_out, 16)
                    sp.wait_ge(y_out, 16 * TILES)
                    sp.wait_ge(unit_staged, TILES)
                    for c in range(RAWS):
                        load(n_pass, 0, c)
                    with sp.Fori(0, TILES) as t:
                        fetch(n_pass, t, CHUNKS - 1, kept_in)
                    for c in range(RAWS, 2 * CHUNKS):
                        if not is_kept(n_pass, c % CHUNKS):
                            load(n_pass, c // CHUNKS, c % CHUNKS)
                with sp.Fori(2 if n_pass == 1 else 0, TILES) as t:
                    for c in range(CHUNKS):
                        if not is_kept(n_pass, c):
                            load(n_pass, t, c)

        @block.gpsimd
        def _(pool):
            for s, v in start_values.items():
                pool.sem_inc(s, v)
            pool.memset(half_power[:, :], -0.5).then_inc(consts_set, 1)
            pool.memset(ident[:, :], 0.0).then_inc(ident_set, 1)
            pool.wait_ge(ident_set, 1)
            pool.affine_select(out=ident[:, :], in_=ident[:, :], compare_op=ALU.not_equal, fill=1.0, base=0,
                               pattern=[[-1, P]], channel_multiplier=1).then_inc(ident_set, 1)

            def inv_root(dst, src, width):
                return pool.tensor_tensor(out=dst, in0=src, in1=half_power[:, 0:1].to_broadcast([P, width]),
                                          op=ALU.pow)

            pool.wait_ge(consts_set, 1)
            pool.wait_ge(uc_summed, BLOCKS // 2)
            inv_root(inv_norm[:, :], squares[:, :], BLOCKS).then_inc(norm_kept, 1)
            pool.wait_ge(norm_kept, 1)
            pool.wait_ge(uc_kept, BLOCKS // 2)
            for t in range(TILES):
                part = xh[:, BPT * t:BPT * (t + 1), P:2 * P]
                scale = inv_norm[:, BPT * t:BPT * (t + 1)].unsqueeze(2).to_broadcast([P, BPT, P])
                pool.tensor_tensor(out=part, in0=part, in1=scale, op=ALU.mult).then_inc(corr_scaled, 1)

            with pool.Fori(0, TILES) as t:
                pool.wait_ge(y_squared, 3 + 3 * t)
                rows = bass.ds(t * BPT, BPT)
                inv_root(inv_norm[:, rows], squares[:, rows], BPT).then_inc(fl_kept, 1)

            mixes = 0
            pool.wait_ge(y_out, 16 * TILES)
            for j in range(BLOCKS + 8):
                q = (j - 11) // BPT
                if (j - 11) % BPT == 0 and 0 <= q < TILES:
                    pool.wait_ge(ln_var, q + 1)
                    inv_root(inv_std[:, :], var_eps[:, :], BPT).then_inc(ln_power, 1)
                    if q in POOL_X1:
                        pool.wait_ge(ln_power, q + 1)
                        for i in range(BPT):
                            block = plane_x[:, q * TW + i * P:q * TW + (i + 1) * P]
                            ins = pool.tensor_scalar(block, block, mean_var[:, 2 * i:2 * i + 1], inv_std[:, i:i + 1],
                                                     ALU.subtract, ALU.mult)
                        ins.then_inc(x1_kept, 1)
                q = (j - 13) // BPT
                if (j - 13) % BPT == 0 and q in POOL_X1:
                    pool.wait_ge(x1_hi, q + 1)
                    nodes = slice(q * TW, (q + 1) * TW)
                    pool.tensor_tensor(out=z_lo[:, nodes], in0=plane_x[:, nodes], in1=z_hi[:, nodes].bitcast(F32),
                                       op=ALU.subtract).then_inc(x1_lo, 1)
                if j < BLOCKS:
                    pool.wait_ge(index_done, 2 + j + 1)
                    for k in range(TOP):
                        pool.indirect_dma_start(
                            gather[:, (j % GATHERS) * TOP + k, :], None, y_dram[:, :],
                            bass.IndirectOffsetOnAxis(ap=top_i[:, j * 8 + k:j * 8 + k + 1], axis=0),
                        ).then_inc(gathered[j], 16)
                m = j - 6
                if 0 <= m < POOL_MIXES:
                    if m % BPT == 0:
                        pool.wait_ge(weight_kept, m // BPT + 1)
                    if m == 0:
                        pool.wait_ge(x_again, 16)
                    pool.wait_ge(gathered[m], 16 * TOP)
                    xm = plane_x[:, m * P:(m + 1) * P]
                    for k in range(TOP):
                        w = weight[:, m * TOP + k:m * TOP + k + 1]
                        pool.tensor_scalar(exp_stage[:, k * P:(k + 1) * P], gather[:, (m % GATHERS) * TOP + k, :],
                                           w, 1.0, ALU.mult, ALU.mult).then_inc(mix_step, 1)
                    for k in range(TOP):
                        pool.wait_ge(mix_step, mixes + TOP + k)
                        s = mixed if k == TOP - 1 else mix_step
                        pool.tensor_tensor(out=xm, in0=xm, in1=exp_stage[:, k * P:(k + 1) * P],
                                           op=ALU.add).then_inc(s, 1)
                    mixes += 2 * TOP - 1
                    pool.wait_ge(mixed, m + 1)

            with pool.Fori(0, TILES) as t:
                pool.wait_ge(x1_kept, t + 1)
                pool.wait_ge(x1_turned, CREDIT + t)
                pool.tensor_copy(turn_stage[:, :], plane_x[:, tile(t)]).then_inc(x1_staged, 1)
            with pool.Fori(0, TILES) as t:
                pool.wait_ge(ln_var, TILES + 1 + t)
                inv_root(inv_std[:, :], var_eps[:, :], BPT)
                mean = cols(mean_var[:, :], 2)[:, :, 0:1].to_broadcast([P, BPT, P])
                pool.tensor_tensor(out=cols(out_stage[:, :]), in0=cols(sum_stage[:, :]), in1=mean,
                                   op=ALU.subtract).then_inc(ln_power, 1)
                pool.wait_ge(ln_power, TILES + 1 + t)
                pool.tensor_tensor(out=cols(out_stage[:, :]), in0=cols(out_stage[:, :]),
                                   in1=inv_std[:, :].unsqueeze(2).to_broadcast([P, BPT, P]),
                                   op=ALU.mult).then_inc(row_out, 1)
                pool.wait_ge(row_out, CREDIT + t + 1)
                pool.dma_start(out[:, tile(t)], out_stage[:, :]).then_inc(stored, 16)
                pool.wait_ge(stored, 16 * t + 16)

        @block.scalar
        def _(act):
            def copy(dst, src):
                return act.activation(dst, src, ACT.Copy)

            def high_part(n_pass, t, c, his):
                wait_chunk(act, n_pass, t, c)
                if n_pass == 1 and isinstance(t, int) and c < SPLITS:
                    act.wait_ge(chunk_used, tile_done(0, TILES - 1))
                else:
                    act.wait_ge(chunk_used, chunk_no(n_pass, t, c) + 1)
                copy(his[c % SPLITS][:, :], raw_chunk(n_pass, t, c)).then_inc(hi_kept, 1)

            for g in range(TILES):
                act.wait_ge(h0_ready, g + 1)
                copy(h0_hi[:, g * TW:(g + 1) * TW], bank(g)).then_inc(h0_split, 1)
            for dst, src in ((whf_s, w_hf), (wq_s, wq), (wk_s, wk), (wv_s, wv), (ffn_s, ffn_w), (ffnb_s, ffn_b),
                             (cheb_s, cheb_w), (chebb_s, cheb_b)):
                act.dma_start(dst[:, :], src).then_inc(loaded, 16)
            for c in range(SPLITS):
                high_part(0, 0, c, hi_front)
            act.wait_ge(gram_ready, 1)
            copy(gram[:, :], bank(6)[:, 0:2 * P]).then_inc(gram_kept, 1)
            for i in range(BLOCKS // 2):
                act.wait_ge(uc_squared, i + 1)
                copy(xh[:, 2 * i:2 * i + 2, P:2 * P], cols(bank(uc_bank(i)), 2 * P)[:, :, P:2 * P]).then_inc(
                    uc_kept, 1)

            def gate_relu_of(tau):
                act.wait_ge(gate_ready, 2 * tau + CREDIT + 1)
                act.wait_ge(y0_kept, CREDIT + tau)
                act.activation(relu_stage[:, :], ps[:, tile(tau)], ACT.Relu).then_inc(gate_relu, 1)

            def y0_of(tau):
                act.wait_ge(y0_kept, CREDIT + tau + 1)
                copy(plane_y[:, tile(tau)], y_stage[:, :]).then_inc(y0_cols, 1)

            def kv0_of(tau):
                act.wait_ge(kv_ready, 2 * tau + CREDIT + 1)
                for h in range(HEADS):
                    copy(k_split[0][h][0:DH, tile(tau)], bank(7)[h * DH:(h + 1) * DH, :]).then_inc(k0_hi, 1)
                act.wait_ge(kv_ready, 2 * tau + CREDIT + 2)
                copy(v_rows[0][:, tile(tau)], ps[:, tile(tau)]).then_inc(v0_kept, 1)

            for c in range(CHUNKS):
                if c >= SPLITS:
                    high_part(0, 0, c, hi_front)
                for i in range(TILES):
                    if c == min(9 + i, CHUNKS - 1):
                        act.wait_ge(corr_turned, i + 1)
                        copy(plane_y[:, i * TW:(i + 1) * TW], bank(2 + i)).then_inc(corr_kept, 1)
            with act.Fori(1, TILES) as t:
                for c in range(CHUNKS):
                    high_part(0, t, c, hi_front)
                    if c == 6:
                        gate_relu_of(t - 1)
                    if c == 10:
                        y0_of(t - 1)
                    if c == 11:
                        kv0_of(t - 1)

            def relu_of(b, tau, job):
                act.wait_ge(side_ready, job + 1)
                act.activation(relu_stage[:, :], bank(7), ACT.Relu, bias=ffnb_s[:, b:b + 1]).then_inc(relu_kept, 1)

            def last_gate_of(job):
                act.wait_ge(side_ready, job + 1)
                act.wait_ge(y0_kept, CREDIT + TILES - 1)
                act.activation(relu_stage[:, :], bank(7), ACT.Relu).then_inc(side_done, 1)

            def unit_hi_of(tau, job):
                act.wait_ge(side_ready, job + 1)
                copy(unit_hi[:, tile(tau)], bank(7)).then_inc(unit_hi_kept, 1)

            def k_hi_of(b, tau, job):
                act.wait_ge(side_ready, job + 1)
                for h in range(HEADS):
                    copy(k_split[b][h][0:DH, tile(tau)], bank(7)[h * DH:(h + 1) * DH, :]).then_inc(k_hi_kept, 1)

            def q_hi_of(t, job):
                act.wait_ge(side_ready, job + 1)
                for h in range(HEADS):
                    for z in range(2):
                        copy(q_hi[h][z * DH:(z + 1) * DH, tile(t)],
                             bank(7)[h * DH:(h + 1) * DH, :]).then_inc(q_hi_kept, 1)

            def tanh_tile(b, t, after):
                for g in range(BLOCKS):
                    s = g % SLOTS
                    act.wait_ge(scores_ready, BLOCKS * (TILES * b + t) + g + 1)
                    act.wait_ge(probs_used, BLOCKS * (TILES * b + t) + g + 1)
                    act.activation(probs[s], ps[:, HEADS * s * TW:HEADS * (s + 1) * TW], ACT.Tanh).then_inc(
                        tanh_done, 1)
                    after(g)

            for b in range(LAYERS):
                if b == 0:
                    q_hi_of(0, 0)

                def first(g):
                    f = last_tile[b]
                    if b == 0 and g == 4:
                        last_gate_of(f)
                    if b == 0 and g == 13:
                        k_hi_of(0, TILES - 1, f + 3)
                    if b == 1 and g == 5:
                        relu_of(0, TILES - 1, f)
                    if b == 1 and g == 9:
                        k_hi_of(1, TILES - 1, f + 1)
                    if g == 19:
                        q_hi_of(1, second_q[b])

                tanh_tile(b, 0, first)

                def tile_t(t):
                    f = job_f(b, t - 1)

                    def later(g):
                        if g == 5:
                            relu_of(b, t - 1, f)
                        if b == 0 and g == 9:
                            k_hi_of(1, t - 1, f + 1)
                        if b == 1 and g == 15:
                            unit_hi_of(t - 1, f + 2)
                        if g == 19 and not isinstance(t, int):
                            q_hi_of(t + 1, f + 3)
                        if g == 19 and isinstance(t, int) and b == 0:
                            q_hi_of(0, first_q[1])

                    tanh_tile(b, t, later)

                with act.Fori(1, TILES - 1) as t:
                    tile_t(t)
                tile_t(TILES - 1)
                if b == 0:
                    act.dma_start(plane_x[:, :], x_rows_d).then_inc(x_again, 16)
            relu_of(1, TILES - 1, last_f)
            def stage_block(j, i):
                for z, unit in enumerate((unit_hi, unit_lo)):
                    ins = copy(block_split[i][:, z * P:(z + 1) * P], unit[:, bass.ds(j * P, P)].bitcast(F32))
                ins.then_inc(block_staged, 1)

            def cos_block(q, i, first=False, last=False):
                for n in range(TILES):
                    if first and n == TILES - 1:
                        unit_hi_of(TILES - 1, last_f + 2)
                    u = TILES * i + n
                    act.wait_ge(cos_ready, BPT * TILES * q + u + 1)
                    if n == 0:
                        act.wait_ge(index_done, BPT * q + i + 1)
                        act.wait_ge(exp_done, BPT * q + i + 1)
                    copy(cos_rows[i % 2][:, n * TW:(n + 1) * TW], bank(u % BANKS)).then_inc(cos_kept, 1)
                if not (last and i >= BPT - 2):
                    stage_block(q * BPT + i + 2, i % 2)
                act.wait_ge(cos_kept, BANKS + BPT * TILES * q + TILES * (i + 1))
                act.wait_ge(exp_done, BPT * q + i + 2)
                act.activation(exp_dump[:, :], cos_rows[i % 2][:, :], ACT.Exp,
                               accum_out=exp_sum[:, bass.ds(BPT * q + i, 1)]).then_inc(exp_done, 1)

            def top_exp(q):
                act.wait_ge(top_done, BPT * q + BPT)
                act.activation(cols(weight_e[:, :], TOP)[:, bass.ds(BPT * q, BPT), :],
                               cols(top_v[:, :], 8)[:, bass.ds(BPT * q, BPT), 0:TOP], ACT.Exp).then_inc(weight_exp, 1)

            def diff_exp(q):
                act.wait_ge(weight_diff, q + 1)
                w = weight_e[:, bass.ds(q * (BPT * TOP), BPT * TOP)]
                act.activation(w, w, ACT.Exp).then_inc(weight_exp, 1)

            def cos_tile(q, last=False):
                for i in range(BPT):
                    cos_block(q, i, last=last)
                    if i == 0:
                        top_exp(q - 1)
                    if i == 1:
                        diff_exp(q - 1)

            act.wait_ge(side_done, job_f(1, 0) + 3)
            stage_block(0, 0)
            stage_block(1, 1)
            for i in range(BPT):
                cos_block(0, i, first=(i == 0))
            with act.Fori(1, TILES - 1) as q:
                cos_tile(q)
            cos_tile(TILES - 1, last=True)

            top_exp(TILES - 1)
            diff_exp(TILES - 1)
            act.wait_ge(index_done, 2 + BLOCKS)

            def a_stage_of(b, tau):
                act.wait_ge(chunk_used, tile_done(1 + 2 * b, tau))
                act.wait_ge(a_turned, CREDIT + TILES * b + tau)
                act.wait_ge(a_cols_kept, CREDIT + TILES * b + tau)
                copy(sum_stage[:, :], ps[:, tile(tau)]).then_inc(a_staged, 1)

            def a_hi_of(b, tau):
                act.wait_ge(a_turned, CREDIT + TILES * b + tau + 1)
                copy(a_hi[:, tile(tau)], bank(6)).then_inc(a_hi_kept, 1)

            def pos_of(b, tau):
                act.wait_ge(chunk_used, tile_done(2 + 2 * b, tau))
                act.wait_ge(h_staged, CREDIT + TILES * b + tau)
                act.activation(relu_stage[:, :], ps[:, tile(tau)], ACT.Relu, bias=chebb_s[:, b:b + 1]).then_inc(pos_kept, 1)

            def exp_of(b, tau):
                act.wait_ge(neg_kept, TILES * b + tau + 1)
                act.activation(exp_stage[:, :], exp_stage[:, :], ACT.Exp).then_inc(exp_kept, 1)

            def h_hi_of(tau):
                act.wait_ge(h_turned, CREDIT + tau + 1)
                copy(z_hi[:, tile(tau)], bank(6)).then_inc(h_hi_kept, 1)

            def chunk_steps(n_pass, t, c, what, b, tau):
                if n_pass > 1 or what:
                    high_part(n_pass, t, c, hi_cheb)
                if what == "a" and c == 3:
                    a_stage_of(b, tau)
                if what == "a" and c == 6:
                    a_hi_of(b, tau)
                if what == "h" and c == 3:
                    pos_of(b, tau)
                if what == "h" and c == 4:
                    exp_of(b, tau)
                if what == "h" and c == 8 and b == 0:
                    h_hi_of(tau)
                if what == "a" and b == 0 and c == 11:
                    act.wait_ge(x1_turned, CREDIT + tau + 1)
                    copy(plane_y[:, tile(tau)], bank(7)).then_inc(x1_cols, 1)

            for n_pass in range(1, 1 + 2 * LAYERS):
                b, half = (n_pass - 1) // 2, (n_pass - 1) % 2
                for c in range(CHUNKS):
                    if half:
                        chunk_steps(n_pass, 0, c, "a", b, TILES - 1)
                    else:
                        chunk_steps(n_pass, 0, c, "h" if b else "", b - 1, TILES - 1)
                first = 2 if n_pass == 1 else 1
                for t in range(1, first):
                    for c in range(CHUNKS):
                        chunk_steps(n_pass, t, c, "ah"[half], b, t - 1)
                with act.Fori(first, TILES) as t:
                    for c in range(CHUNKS):
                        chunk_steps(n_pass, t, c, "ah"[half], b, t - 1)
            pos_of(LAYERS - 1, TILES - 1)
            exp_of(LAYERS - 1, TILES - 1)

        @block.tensor
        def _(pe):
            def adj_chunk(n_pass, t, c, zh, zl, his, los):
                pe.wait_ge(lo_kept, RAWS + split_no(n_pass, t, c) + 1)
                hi, lo = his[c % SPLITS], los[c % SPLITS]
                for i in range(CH):
                    j = c * CH + i
                    zj = slice(j * P, (j + 1) * P)
                    part = slice(i * TW, (i + 1) * TW)
                    dst = ps[:, tile(t)]
                    pe.matmul(dst, zh[:, zj], hi[:, part], start=(j == 0), stop=False)
                    pe.matmul(dst, zh[:, zj], lo[:, part], start=False, stop=False)
                    mm = pe.matmul(dst, zl[:, zj], hi[:, part], start=False, stop=(j == BLOCKS - 1))
                mm.then_inc(chunk_used, 1)

            def whole_chunk(n_pass, t, c):
                wait_chunk(pe, n_pass, t, c)
                for j in range(c * CH, (c + 1) * CH):
                    mm = pe.matmul(ps[:, tile(t)], plane_x[:, j * P:(j + 1) * P],
                                   raw_chunk(n_pass, t, c)[:, (j % CH) * TW:(j % CH + 1) * TW],
                                   start=(j == 0), stop=(j == BLOCKS - 1))
                mm.then_inc(chunk_used, 1)

            def turn(dst, src):
                for q in range(BPT):
                    mm = pe.transpose(dst[:, q * P:(q + 1) * P], src[:, q * P:(q + 1) * P], ident[:, :])
                return mm

            pe.wait_ge(loaded_first, 16)
            for j in range(BLOCKS):
                if j % BPT == 0:
                    pe.wait_ge(x_in[j // BPT], 16)
                mm = pe.matmul(ps[:, j * P:(j + 1) * P], plane_x[:, j * P:(j + 1) * P], wh_s[:, 0:P],
                               start=True, stop=True)
                if j % BPT == BPT - 1:
                    mm.then_inc(h0_ready, 1)
            pe.wait_ge(rows_in, 16)
            for j in range(BLOCKS):
                if j % BPT == 0:
                    pe.wait_ge(h0_kept, j // BPT + 1)
                mm = pe.matmul(bank(6)[:, 0:2 * P], xh[:, j, 0:P], xh[:, j, :], start=(j == 0), stop=(j == BLOCKS - 1))
            mm.then_inc(gram_ready, 1)
            pe.wait_ge(gram_kept, 1)
            for i in range(BLOCKS // 2):
                if i >= UC_BANKS:
                    pe.wait_ge(uc_kept, i - UC_BANKS + 1)
                for k in range(2):
                    j = 2 * i + k
                    mm = pe.matmul(bank(uc_bank(i))[:, k * 2 * P:(k + 1) * 2 * P], plane_x[:, j * P:(j + 1) * P], gram[:, :],
                                   start=True, stop=True)
                mm.then_inc(uc_ready, 1)

            def gate_of(tau):
                pe.wait_ge(agg_kept, tau + 1)
                pe.matmul(ps[:, tile(tau)], wh_s[:, P:2 * P], plane_x[:, tile(tau)], start=True, stop=False)
                pe.matmul(ps[:, tile(tau)], whf_s[:, 0:P], sum_stage[:, :], start=False, stop=True).then_inc(
                    gate_ready, 1)
                pe.wait_ge(k0_lo, 2 * tau + CREDIT)
                pe.matmul(bank(7), whf_s[:, P:2 * P], sum_stage[:, :], start=True, stop=True).then_inc(gate_ready, 1)

            def h2_of(tau):
                pe.wait_ge(gate_relu, tau + 1)
                pe.matmul(ps[:, tile(tau)], wh_s[:, 2 * P:3 * P], plane_x[:, tile(tau)], start=True,
                          stop=True).then_inc(h2_ready, 1)

            def kv0_of(tau):
                pe.wait_ge(y0_kept, CREDIT + tau + 1)
                pe.matmul(bank(7), wk_s[:, 0:P], y_stage[:, :], start=True, stop=True).then_inc(kv_ready, 1)
                for q in range(BPT):
                    mm = pe.matmul(ps[:, bass.ds(tau * TW + q * P, P)], y_stage[:, q * P:(q + 1) * P], wv_s[:, 0:P],
                                   start=True, stop=True)
                mm.then_inc(kv_ready, 1)

            front = (h0_hi, h0_lo, hi_front, lo_front)
            pe.wait_ge(loaded, 16 * 8)
            pe.wait_ge(ident_set, 2)
            for c in range(CHUNKS):
                i = c - 5
                if 0 <= i < TILES:
                    pe.wait_ge(uc_kept, BLOCKS // 2)
                    pe.wait_ge(corr_scaled, i + 1)
                    for q in range(BPT):
                        mm = pe.transpose(bank(2 + i)[:, q * P:(q + 1) * P], xh[:, BPT * i + q, P:2 * P], ident[:, :])
                    mm.then_inc(corr_turned, 1)
                adj_chunk(0, 0, c, *front)
            pe.wait_ge(corr_kept, TILES)
            with pe.Fori(1, TILES) as t:
                for c in range(CHUNKS):
                    if c == 2:
                        gate_of(t - 1)
                    if c == 6:
                        h2_of(t - 1)
                    if c == 9:
                        kv0_of(t - 1)
                    adj_chunk(0, t, c, *front)

            def score(b, t, g):
                pe.wait_ge(tanh_done, BLOCKS * (TILES * b + t) + g + 1)
                for h in range(HEADS):
                    dst = bank(HEADS * (g % SLOTS) + h)
                    kb = k_split[b][h][:, g * P:(g + 1) * P]
                    pe.matmul(dst, kb, q_hi[h][:, tile(t)], start=True, stop=False)
                    mm = pe.matmul(dst, kb, q_lo[h][:, tile(t)], start=False, stop=True)
                mm.then_inc(scores_ready, 1)

            def weigh(b, t, g):
                pe.wait_ge(tanh_done, SLOTS + BLOCKS * (TILES * b + t) + g + 1)
                for h in range(HEADS):
                    mm = pe.matmul(bank(6)[h * DH:(h + 1) * DH, :],
                                   v_rows[b][:, g * P + h * DH:g * P + (h + 1) * DH],
                                   probs[g % SLOTS][:, h * TW:(h + 1) * TW],
                                   start=(g == 0), stop=(g == BLOCKS - 1))
                mm.then_inc(probs_used, 1)

            def feed(b, tau, job):
                pe.wait_ge(att_kept, CREDIT + TILES * b + tau + 1)
                pe.wait_ge(side_done, job)
                pe.matmul(bank(7), ffn_s[:, b * P:(b + 1) * P], sum_stage[:, :], start=True, stop=True).then_inc(
                    side_ready, 1)

            def last_gate(job):
                pe.wait_ge(side_done, job)
                pe.matmul(bank(7), wh_s[:, P:2 * P], plane_x[:, N - TW:N], start=True, stop=False)
                pe.matmul(bank(7), whf_s[:, 0:P], sum_stage[:, :], start=False, stop=True).then_inc(side_ready, 1)

            def last_f1(job):
                pe.wait_ge(side_done, job)
                pe.matmul(bank(7), whf_s[:, P:2 * P], sum_stage[:, :], start=True, stop=True).then_inc(side_ready, 1)

            def last_h2(job):
                pe.wait_ge(side_done, job)
                pe.matmul(bank(7), wh_s[:, 2 * P:3 * P], plane_x[:, N - TW:N], start=True, stop=True).then_inc(
                    side_ready, 1)

            def keys(b, job):
                pe.wait_ge(side_done, job)
                pe.matmul(bank(7), wk_s[:, b * P:(b + 1) * P], y_stage[:, :], start=True, stop=True).then_inc(side_ready, 1)

            def values(b, job):
                pe.wait_ge(side_done, job)
                for q in range(BPT):
                    mm = pe.matmul(bank(7)[:, q * P:(q + 1) * P], y_stage[:, q * P:(q + 1) * P], wv_s[:, b * P:(b + 1) * P],
                                   start=True, stop=True)
                mm.then_inc(side_ready, 1)

            def queries(b, t, job):
                if not isinstance(job, int) or job > 0:
                    pe.wait_ge(side_done, job)
                pe.matmul(bank(7), wq_s[:, b * P:(b + 1) * P], plane_y[:, tile(t)], start=True, stop=True).then_inc(
                    side_ready, 1)

            def y_to_rows(job):
                pe.wait_ge(side_done, job)
                turn(bank(7), y_stage).then_inc(side_ready, 1)

            def unit_to_columns(tau, job):
                pe.wait_ge(unit_staged, tau + 1)
                pe.wait_ge(side_done, job)
                turn(bank(7), turn_stage).then_inc(side_ready, 1)

            pe.wait_ge(agg_kept, TILES)
            pe.wait_ge(k0_lo, 2 * (TILES - 1) + CREDIT)
            pe.wait_ge(v0_kept, TILES - 1)
            pe.wait_ge(y0_cols, CREDIT + TILES - 1)
            for b in range(LAYERS):
                if b == 0:
                    queries(0, 0, 0)
                pe.wait_ge(side_done, first_q[b] + 1)
                score(b, 0, 0)
                score(b, 0, 1)
                for g in range(0, BLOCKS, 2):
                    f = last_tile[b]
                    if b == 0:
                        if g == 2:
                            last_gate(f)
                        if g == 6:
                            last_f1(f + 1)
                        if g == 8:
                            last_h2(f + 2)
                        if g == 10:
                            keys(0, f + 3)
                        if g == 14:
                            values(0, f + 4)
                    else:
                        if g == 2:
                            feed(0, TILES - 1, f)
                        if g == 6:
                            keys(1, f + 1)
                        if g == 10:
                            values(1, f + 2)
                    if g == 16:
                        queries(b, 1, second_q[b])
                    if g + 2 < BLOCKS:
                        if g + 2 == BLOCKS - BPT:
                            pe.wait_ge(side_done, second_q[b])
                        score(b, 0, g + 2)
                        score(b, 0, g + 3)
                    if g == 0:
                        pe.wait_ge(att_kept, CREDIT + TILES * b)
                    weigh(b, 0, g)
                    weigh(b, 0, g + 1)

                def tile_t(t):
                    f = job_f(b, t - 1)
                    pe.wait_ge(side_done, f)
                    score(b, t, 0)
                    score(b, t, 1)
                    for g in range(0, BLOCKS, 2):
                        if g == 2:
                            feed(b, t - 1, f)
                        if g == 6 and b == 0:
                            keys(1, f + 1)
                        if g == 6 and b == 1:
                            y_to_rows(f + 1)
                        if g == 10 and b == 0:
                            values(1, f + 2)
                        if g == 12 and b == 1:
                            unit_to_columns(t - 1, f + 2)
                        if g == 16 and not isinstance(t, int):
                            queries(b, t + 1, f + 3)
                        if g == 16 and isinstance(t, int) and b == 0:
                            queries(1, 0, first_q[1])
                        if g + 2 < BLOCKS:
                            score(b, t, g + 2)
                            score(b, t, g + 3)
                        if g == 0:
                            pe.wait_ge(att_kept, CREDIT + TILES * b + t)
                        weigh(b, t, g)
                        weigh(b, t, g + 1)

                with pe.Fori(1, TILES - 1) as t:
                    tile_t(t)
                tile_t(TILES - 1)

            def cosines(q, i, tiles):
                hi, lo = block_split[i % 2][:, 0:P], block_split[i % 2][:, P:2 * P]
                for n in tiles:
                    u = TILES * i + n
                    pe.wait_ge(cos_kept, BPT * TILES * q + u + 1)
                    nodes = slice(n * TW, (n + 1) * TW)
                    dst = bank(u % BANKS)
                    pe.matmul(dst, hi, unit_hi[:, nodes], start=True, stop=False)
                    pe.matmul(dst, hi, unit_lo[:, nodes], start=False, stop=False)
                    pe.matmul(dst, lo, unit_hi[:, nodes], start=False, stop=True).then_inc(cos_ready, 1)

            feed(1, TILES - 1, last_f)
            pe.wait_ge(tanh_done, SLOTS + LAYERS * TILES * BLOCKS)
            pe.wait_ge(block_staged, 1)
            cosines(0, 0, range(2))
            y_to_rows(last_f + 1)
            cosines(0, 0, range(2, TILES - 1))
            unit_to_columns(TILES - 1, last_f + 2)
            pe.wait_ge(side_done, last_side)
            cosines(0, 0, [TILES - 1])
            for i in range(1, BPT):
                pe.wait_ge(block_staged, i + 1)
                cosines(0, i, range(TILES))
            with pe.Fori(1, TILES) as q:
                for i in range(BPT):
                    pe.wait_ge(block_staged, BPT * q + i + 1)
                    cosines(q, i, range(TILES))

            pe.wait_ge(cos_kept, BANKS + BLOCKS * TILES)
            pe.wait_ge(weights_mixed, 1)

            def a_rows(b, tau):
                pe.wait_ge(a_staged, TILES * b + tau + 1)
                pe.wait_ge(a_lo_kept, CREDIT + TILES * b + tau)
                for q in range(BPT):
                    mm = pe.matmul(bank(6)[:, q * P:(q + 1) * P], sum_stage[:, q * P:(q + 1) * P],
                                   cheb_mix[:, (2 * b + 1) * P:(2 * b + 2) * P], start=True, stop=True)
                mm.then_inc(a_turned, 1)

            def near_terms(b, t):
                if b == 0:
                    pe.wait_ge(x1_cols, CREDIT + t + 1)
                if isinstance(t, int):
                    pe.wait_ge(a_cols_kept, CREDIT + TILES * (b + 1))
                dst = ps[:, tile(t)]
                pe.matmul(dst, cheb_mix[:, 2 * b * P:(2 * b + 1) * P], plane_y[:, tile(t)], start=False, stop=False)
                pe.matmul(dst, cheb_s[:, (b * 3 + 1) * P:(b * 3 + 2) * P], a_cols[:, tile(t)], start=False, stop=False)

            def turn_h(b, tau):
                pe.wait_ge(h_staged, CREDIT + TILES * b + tau + 1)
                pe.wait_ge(h_lo_kept, CREDIT + TILES * b + tau)
                turn(bank(6), turn_stage).then_inc(h_turned, 1)

            def chunk_steps(n_pass, t, c, what, b, tau, *z):
                if what == "a" and c == 2:
                    a_rows(b, tau)
                if what == "h" and c == 4:
                    turn_h(b, tau)
                if n_pass % 2 == 0 and c == 8:
                    near_terms((n_pass - 1) // 2, t)
                if what == "a" and b == 0 and c == 7:
                    pe.wait_ge(x1_staged, tau + 1)
                    pe.wait_ge(x1_cols, CREDIT + tau)
                    turn(bank(7), turn_stage).then_inc(x1_turned, 1)
                if n_pass > 1 or what:
                    adj_chunk(n_pass, t, c, *z)
                else:
                    whole_chunk(n_pass, t, c)

            for n_pass in range(1, 1 + 2 * LAYERS):
                b, half = (n_pass - 1) // 2, (n_pass - 1) % 2
                z = (a_hi, a_lo, hi_cheb, lo_cheb) if half else (z_hi, z_lo, hi_cheb, lo_cheb)
                for c in range(CHUNKS):
                    if c % (BPT // CH) == 0:
                        z_tile = c // (BPT // CH)
                        if half:
                            pe.wait_ge(a_lo_kept, CREDIT + TILES * b + z_tile + 1)
                        elif b:
                            pe.wait_ge(h_lo_kept, CREDIT + z_tile + 1)
                        else:
                            pe.wait_ge(x1_kept, z_tile + 1)
                    what = ("a", b, TILES - 1) if half else ("h" if b else "", b - 1, TILES - 1)
                    chunk_steps(n_pass, 0, c, *what, *z)
                if n_pass == 1:
                    pe.wait_ge(x1_lo, TILES)
                with pe.Fori(1, TILES) as t:
                    for c in range(CHUNKS):
                        chunk_steps(n_pass, t, c, "ah"[half], b, t - 1, *z)
            turn_h(LAYERS - 1, TILES - 1)

        @block.vector
        def _(dve):
            def copy(dst, src):
                return dve.tensor_scalar(dst, src, 1.0, None, ALU.mult)

            def sub(dst, a, b):
                return dve.tensor_tensor(out=dst, in0=a, in1=b.bitcast(F32), op=ALU.subtract)

            def low_part(n_pass, t, c, his, los):
                dve.wait_ge(hi_kept, split_no(n_pass, t, c) + 1)
                sub(los[c % SPLITS][:, :], raw_chunk(n_pass, t, c), his[c % SPLITS][:, :]).then_inc(lo_kept, 1)

            for g in range(TILES):
                dve.wait_ge(h0_split, g + 1)
                sub(h0_lo[:, g * TW:(g + 1) * TW], bank(g), h0_hi[:, g * TW:(g + 1) * TW])
                copy(xh[:, g * BPT:(g + 1) * BPT, P:2 * P], cols(bank(g))).then_inc(h0_kept, 1)
            for c in range(SPLITS):
                low_part(0, 0, c, hi_front, lo_front)
            for i in range(BLOCKS // 2):
                dve.wait_ge(uc_ready, i + 1)
                if i:
                    dve.wait_ge(uc_summed, i)
                prod = cols(exp_stage[:, 0:2 * P])
                dve.tensor_tensor(out=prod, in0=cols(bank(uc_bank(i)), 2 * P)[:, :, 0:P], in1=xh[:, 2 * i:2 * i + 2, 0:P],
                                  op=ALU.mult).then_inc(uc_squared, 1)
                dve.wait_ge(uc_squared, i + 1)
                dve.tensor_reduce(squares[:, 2 * i:2 * i + 2], prod, AX_X, ALU.add).then_inc(uc_summed, 1)

            def agg_of(tau):
                dve.wait_ge(gate_ready, 2 * tau + CREDIT)
                dve.wait_ge(chunk_used, tile_done(0, tau))
                dve.tensor_tensor(out=sum_stage[:, :], in0=ps[:, tile(tau)], in1=plane_y[:, tile(tau)],
                                  op=ALU.add).then_inc(agg_kept, 1)

            def gate_of(tau):
                dve.wait_ge(gate_ready, 2 * tau + CREDIT + 2)
                dve.wait_ge(gate_relu, tau + 1)
                dve.tensor_tensor(out=relu_stage[:, :], in0=bank(7), in1=relu_stage[:, :], op=ALU.mult).then_inc(
                    gated, 1)

            def y0_of(tau):
                dve.wait_ge(h2_ready, tau + 1)
                dve.wait_ge(gated, tau + 1)
                dve.wait_ge(kv_ready, 2 * tau + CREDIT)
                dve.wait_ge(y0_cols, CREDIT + tau)
                dve.tensor_tensor(out=y_stage[:, :], in0=ps[:, tile(tau)], in1=relu_stage[:, :], op=ALU.add).then_inc(
                    y0_kept, 1)

            def k0_lo_of(tau):
                for h in range(HEADS):
                    dve.wait_ge(k0_hi, 2 * tau + h + 1)
                    k = k_split[0][h]
                    sub(k[DH:P, tile(tau)], bank(7)[h * DH:(h + 1) * DH, :], k[0:DH, tile(tau)]).then_inc(k0_lo, 1)

            for c in range(SPLITS, CHUNKS):
                low_part(0, 0, c, hi_front, lo_front)
            dve.wait_ge(corr_kept, TILES)
            with dve.Fori(1, TILES) as t:
                for c in range(CHUNKS):
                    low_part(0, t, c, hi_front, lo_front)
                    if c == 3:
                        agg_of(t - 1)
                    if c == 6:
                        gate_of(t - 1)
                    if c == 9:
                        y0_of(t - 1)
                    if c == 11:
                        k0_lo_of(t - 1)
            agg_of(TILES - 1)

            dve.wait_ge(loaded, 16 * 8)

            def att_of(b, tau):
                dve.wait_ge(probs_used, SLOTS + BLOCKS * (TILES * b + 1) + tau * BLOCKS)
                copy(sum_stage[:, :], bank(6)).then_inc(att_kept, 1)

            def y_of(b, tau):
                dve.wait_ge(relu_kept, TILES * b + tau + 1)
                dve.tensor_tensor(out=y_stage[:, :], in0=plane_y[:, tile(tau)], in1=relu_stage[:, :],
                                  op=ALU.add).then_inc(side_done, 1)

            def k_lo_of(b, tau, n):
                for h in range(HEADS):
                    dve.wait_ge(k_hi_kept, 2 * n + h + 1)
                    k = k_split[b][h]
                    ins = sub(k[DH:P, tile(tau)], bank(7)[h * DH:(h + 1) * DH, :], k[0:DH, tile(tau)])
                ins.then_inc(side_done, 1)

            def v_of(b, tau, job):
                dve.wait_ge(side_ready, job + 1)
                copy(v_rows[b][:, tile(tau)], bank(7)).then_inc(side_done, 1)

            def q_lo_of(t, n):
                for h in range(HEADS):
                    dve.wait_ge(q_hi_kept, 4 * n + 2 * h + 2)
                    for z in range(2):
                        part = slice(z * DH, (z + 1) * DH)
                        ins = sub(q_lo[h][part, tile(t)], bank(7)[h * DH:(h + 1) * DH, :], q_hi[h][part, tile(t)])
                ins.then_inc(side_done, 1)

            def rows_of(tau, job):
                dve.wait_ge(side_ready, job + 1)
                copy(y_rows[:, tile(tau)], bank(7)).then_inc(side_done, 1)
                dve.wait_ge(side_done, job + 1)
                dve.tensor_tensor(out=exp_stage[:, :], in0=y_rows[:, tile(tau)], in1=y_rows[:, tile(tau)],
                                  op=ALU.mult).then_inc(y_squared, 1)
                dve.wait_ge(y_squared, 3 * tau + 1)
                sums = squares[:, bass.ds(BPT * tau, BPT)]
                dve.tensor_reduce(sums, cols(exp_stage[:, :]), AX_X, ALU.add).then_inc(y_squared, 1)
                dve.wait_ge(y_squared, 3 * tau + 2)
                dve.tensor_scalar(sums, sums, P * 1e-6, None, ALU.add).then_inc(y_squared, 1)

            def unit_of(tau, job):
                dve.wait_ge(fl_kept, tau + 1)
                scale = inv_norm[:, bass.ds(BPT * tau, BPT)].unsqueeze(2).to_broadcast([P, BPT, P])
                dve.tensor_tensor(out=cols(turn_stage[:, :]), in0=cols(y_rows[:, tile(tau)]), in1=scale,
                                  op=ALU.mult).then_inc(unit_staged, 1)
                dve.wait_ge(unit_hi_kept, tau + 1)
                sub(unit_lo[:, tile(tau)], bank(7), unit_hi[:, tile(tau)]).then_inc(side_done, 1)

            def y_to_columns(tau, job):
                dve.wait_ge(side_done, job + 1)
                copy(plane_y[:, tile(tau)], y_stage[:, :])

            for b in range(LAYERS):
                if b == 0:
                    q_lo_of(0, 0)
                f = last_tile[b]
                if b == 0:
                    dve.wait_ge(side_ready, f + 2)
                    dve.wait_ge(side_done, f + 1)
                    dve.tensor_tensor(out=relu_stage[:, :], in0=bank(7), in1=relu_stage[:, :], op=ALU.mult).then_inc(
                        side_done, 1)
                    dve.wait_ge(side_ready, f + 3)
                    dve.wait_ge(side_done, f + 2)
                    dve.wait_ge(kv_ready, 2 * (TILES - 1) + CREDIT)
                    dve.wait_ge(y0_cols, CREDIT + TILES - 1)
                    dve.tensor_tensor(out=y_stage[:, :], in0=bank(7), in1=relu_stage[:, :], op=ALU.add).then_inc(
                        side_done, 1)
                    y_to_columns(TILES - 1, f + 2)
                    k_lo_of(0, TILES - 1, 0)
                    v_of(0, TILES - 1, f + 4)
                else:
                    att_of(0, TILES - 1)
                    y_of(0, TILES - 1)
                    y_to_columns(TILES - 1, f)
                    k_lo_of(1, TILES - 1, TILES)
                    v_of(1, TILES - 1, f + 2)
                q_lo_of(1, TILES * b + 1)

                def tile_t(t):
                    f = job_f(b, t - 1)
                    att_of(b, t - 1)
                    y_of(b, t - 1)
                    if b == 0:
                        y_to_columns(t - 1, f)
                        k_lo_of(1, t - 1, t)
                        v_of(1, t - 1, f + 2)
                    else:
                        rows_of(t - 1, f + 1)
                        unit_of(t - 1, f + 2)
                    if not isinstance(t, int):
                        q_lo_of(t + 1, TILES * b + t + 1)
                    elif b == 0:
                        q_lo_of(0, TILES)

                with dve.Fori(1, TILES - 1) as t:
                    tile_t(t)
                tile_t(TILES - 1)
            att_of(1, TILES - 1)
            y_of(1, TILES - 1)
            rows_of(TILES - 1, last_f + 1)
            unit_of(TILES - 1, last_f + 2)

            for b in range(LAYERS):
                w0, w2 = (cheb_s[:, (3 * b + k) * P:(3 * b + k + 1) * P] for k in (0, 2))
                dve.tensor_tensor(out=cheb_mix[:, 2 * b * P:(2 * b + 1) * P], in0=w0, in1=w2, op=ALU.subtract)
                ins = dve.tensor_scalar(cheb_mix[:, (2 * b + 1) * P:(2 * b + 2) * P], w2, 2.0, None, ALU.mult)
            ins.then_inc(weights_mixed, 1)

            def per_block(ap, q, n):
                return ap[:, BPT * q:BPT * (q + 1)].unsqueeze(2).to_broadcast([P, BPT, n])

            def of_tile(ap, q):
                return cols(ap[:, :], TOP)[:, BPT * q:BPT * (q + 1), :]

            steps = 0

            def shares(q):
                nonlocal steps
                dve.wait_ge(exp_done, 2 + BPT * (q + 1))
                r = exp_sum[:, BPT * q:BPT * (q + 1)]
                dve.reciprocal(r, r).then_inc(weight_step, 1)
                dve.wait_ge(weight_step, steps + 1)
                dve.wait_ge(weight_exp, 2 * q + 1)
                dve.tensor_tensor(out=of_tile(weight_p, q), in0=of_tile(weight_e, q), in1=per_block(exp_sum, q, TOP),
                                  op=ALU.mult).then_inc(weight_step, 1)
                dve.wait_ge(weight_step, steps + 2)
                steps += 2
                first = of_tile(weight_p, q)[:, :, 0:1].to_broadcast([P, BPT, TOP])
                dve.tensor_tensor(out=of_tile(weight_e, q), in0=of_tile(weight_p, q), in1=first,
                                  op=ALU.subtract).then_inc(weight_diff, 1)

            def weights(q):
                nonlocal steps
                dve.wait_ge(weight_exp, 2 * q + 2)
                r = exp_sum[:, BPT * q:BPT * (q + 1)]
                dve.tensor_reduce(r, of_tile(weight_e, q), AX_X, ALU.add).then_inc(weight_step, 1)
                dve.wait_ge(weight_step, steps + 1)
                dve.reciprocal(r, r).then_inc(weight_step, 1)
                dve.wait_ge(weight_step, steps + 2)
                steps += 2
                dve.tensor_tensor(out=of_tile(weight, q), in0=of_tile(weight_e, q), in1=per_block(exp_sum, q, TOP),
                                  op=ALU.mult).then_inc(weight_kept, 1)

            ln_steps = 2 * BPT

            def variances(src, before):
                for i in range(BPT):
                    dve.bn_stats(stats[:, 6 * i:6 * i + 6], src[:, i * P:(i + 1) * P]).then_inc(ln_step, 1)
                dve.wait_ge(ln_step, before + BPT)
                dve.memset(var_eps[:, :], 1e-5)
                for i in range(BPT):
                    dve.bn_aggr(mean_var[:, 2 * i:2 * i + 2], stats[:, 6 * i:6 * i + 6]).then_inc(ln_step, 1)
                dve.wait_ge(ln_step, before + ln_steps)
                dve.tensor_tensor(out=var_eps[:, :], in0=var_eps[:, :], in1=cols(mean_var[:, :], 2)[:, :, 1],
                                  op=ALU.add).then_inc(ln_var, 1)

            def normal(dst, src, i):
                return dve.tensor_scalar(dst[:, i * P:(i + 1) * P], src[:, i * P:(i + 1) * P],
                                         mean_var[:, 2 * i:2 * i + 1], inv_std[:, i:i + 1], ALU.subtract, ALU.mult)

            def find_top(j):
                dve.wait_ge(cos_kept, BANKS + TILES * (j + 1))
                top = top_v[:, j * 8:(j + 1) * 8]
                dve.max(top, cos_rows[j % 2][:, :]).then_inc(top_done, 1)
                dve.wait_ge(top_done, j + 1)
                dve.max_index(top_i[:, j * 8:(j + 1) * 8], top, cos_rows[j % 2][:, :]).then_inc(index_done, 1)

            def x1_of(q):
                nodes = slice(q * TW, (q + 1) * TW)
                if q not in POOL_X1:
                    dve.wait_ge(ln_power, q + 1)
                    for i in range(BPT):
                        ins = normal(plane_x[:, nodes], plane_x[:, nodes], i)
                    ins.then_inc(x1_kept, 1)
                dve.wait_ge(x1_kept, q + 1)
                copy(z_hi[:, nodes], plane_x[:, nodes]).then_inc(x1_hi, 1)
                dve.wait_ge(x1_hi, q + 1)
                if q not in POOL_X1:
                    sub(z_lo[:, nodes], plane_x[:, nodes], z_hi[:, nodes]).then_inc(x1_lo, 1)

            def mix_rows(first, end, before):
                for k in range(TOP):
                    if k:
                        dve.wait_ge(mix_last_step, before + k)
                    for m in range(first, end):
                        if k == 0:
                            dve.wait_ge(gathered[m], 16 * TOP)
                        xm = plane_x[:, m * P:(m + 1) * P]
                        ins = dve.scalar_tensor_tensor(
                            out=xm, in0=gather[:, (m % GATHERS) * TOP + k, :],
                            scalar=weight[:, m * TOP + k:m * TOP + k + 1], in1=xm, op0=ALU.mult, op1=ALU.add)
                    ins.then_inc(mix_last_step, 1)
                dve.wait_ge(mix_last_step, before + TOP)

            def after_top(j):
                def due(lag):
                    return (j - lag) % BPT == 0 and 0 <= (j - lag) // BPT < TILES

                if due(4):
                    shares((j - 4) // BPT)
                if due(5):
                    weights((j - 5) // BPT)
                if j == BLOCKS + 1:
                    dve.wait_ge(weight_kept, TILES)
                    mix_rows(POOL_MIXES, BLOCKS - BPT, 0)
                if due(10):
                    q = (j - 10) // BPT
                    dve.wait_ge(mixed, min(BPT * (q + 1), POOL_MIXES))
                    variances(plane_x[:, q * TW:(q + 1) * TW], q * ln_steps)
                if j == BLOCKS + 2:
                    mix_rows(BLOCKS - BPT, BLOCKS, TOP)
                for q in range(TILES):
                    if j == BPT * q + (12 if q in POOL_X1 else 11):
                        x1_of(q)

            for j in range(BLOCKS):
                find_top(j)
                after_top(j)
            for j in range(BLOCKS, BLOCKS + 8):
                after_top(j)

            def a_cols_of(b, tau):
                dve.wait_ge(a_staged, TILES * b + tau + 1)
                copy(a_cols[:, tile(tau)], sum_stage[:, :]).then_inc(a_cols_kept, 1)

            def a_lo_of(b, tau):
                dve.wait_ge(a_hi_kept, TILES * b + tau + 1)
                sub(a_lo[:, tile(tau)], bank(6), a_hi[:, tile(tau)]).then_inc(a_lo_kept, 1)

            def neg_of(b, tau):
                dve.wait_ge(pos_kept, TILES * b + tau + 1)
                dve.tensor_scalar(exp_stage[:, :], ps[:, tile(tau)], chebb_s[:, b:b + 1], 0.0, ALU.add, ALU.min).then_inc(
                    neg_kept, 1)

            def h_of(b, tau):
                dve.wait_ge(exp_kept, TILES * b + tau + 1)
                dve.wait_ge(h_turned, CREDIT + TILES * b + tau)
                dve.scalar_tensor_tensor(out=turn_stage[:, :], in0=exp_stage[:, :], scalar=-1.0, in1=relu_stage[:, :],
                                         op0=ALU.add, op1=ALU.add).then_inc(h_staged, 1)
                if b == 0:
                    dve.wait_ge(h_staged, CREDIT + tau + 1)
                    copy(plane_y[:, tile(tau)], turn_stage[:, :])

            def h_lo_of(tau):
                dve.wait_ge(h_hi_kept, tau + 1)
                sub(z_lo[:, tile(tau)], bank(6), z_hi[:, tile(tau)]).then_inc(h_lo_kept, 1)

            def result_sum(tau):
                dve.wait_ge(h_turned, CREDIT + TILES * (LAYERS - 1) + tau + 1)
                dve.wait_ge(row_out, CREDIT + tau)
                dve.tensor_tensor(out=sum_stage[:, :], in0=bank(6), in1=plane_x[:, tile(tau)], op=ALU.add).then_inc(
                    h_lo_kept, 1)
                dve.wait_ge(h_lo_kept, CREDIT + TILES * (LAYERS - 1) + tau + 1)
                variances(sum_stage, TILES * ln_steps + tau * ln_steps)

            def chunk_steps(n_pass, t, c, what, b, tau):
                if n_pass > 1 or what:
                    low_part(n_pass, t, c, hi_cheb, lo_cheb)
                if what == "a" and c == 4:
                    a_cols_of(b, tau)
                if what == "a" and c == 7:
                    a_lo_of(b, tau)
                if what == "h" and c == 3:
                    neg_of(b, tau)
                if what == "h" and c == 4:
                    h_of(b, tau)
                if what == "h" and c == 8:
                    if b == 0:
                        h_lo_of(tau)
                    else:
                        result_sum(tau)

            for n_pass in range(1, 1 + 2 * LAYERS):
                b, half = (n_pass - 1) // 2, (n_pass - 1) % 2
                for c in range(CHUNKS):
                    if half:
                        chunk_steps(n_pass, 0, c, "a", b, TILES - 1)
                    else:
                        chunk_steps(n_pass, 0, c, "h" if b else "", b - 1, TILES - 1)
                with dve.Fori(1, TILES) as t:
                    for c in range(CHUNKS):
                        chunk_steps(n_pass, t, c, "ah"[half], b, t - 1)
            neg_of(LAYERS - 1, TILES - 1)
            h_of(LAYERS - 1, TILES - 1)
            result_sum(TILES - 1)


def kernel(x, adj, L0_gnn_w_h, L0_gnn_w_hf, L0_gnn_wq, L0_gnn_wk, L0_gnn_wv, L0_gnn_ffn_w, L0_gnn_ffn_b,
           L1_gnn_W0, L1_gnn_b0, L1_gnn_W1, L1_gnn_b1):
    import numpy as np
    import concourse.bacc as bacc
    from concourse.bass_utils import run_bass_kernel_spmd

    def rows(a):
        a = np.asarray(a)
        return a.reshape(-1, P, a.shape[-1]).transpose(1, 0, 2).reshape(P, -1)

    def side(w):
        return np.asarray(w).transpose(2, 0, 1).reshape(P, -1)

    adj_t = np.asarray(adj).reshape(TILES, TW, BLOCKS, P).transpose(3, 0, 2, 1).reshape(P, -1)
    cheb = np.concatenate([np.asarray(L1_gnn_W0), np.asarray(L1_gnn_W1)], axis=0)
    arrays = {
        "x_rows": rows(x),
        "x_cols": np.asarray(x).T,
        "adj_t": adj_t,
        "w_h": np.asarray(L0_gnn_w_h).T,
        "w_hf": np.asarray(L0_gnn_w_hf).T,
        "wq": side(L0_gnn_wq),
        "wk": side(L0_gnn_wk),
        "wv": side(L0_gnn_wv),
        "ffn_w": side(L0_gnn_ffn_w),
        "ffn_b": np.asarray(L0_gnn_ffn_b).T,
        "cheb_w": cheb.transpose(1, 0, 2).reshape(P, -1),
        "cheb_b": np.stack([np.asarray(L1_gnn_b0), np.asarray(L1_gnn_b1)], axis=1),
    }
    arrays = {k: np.ascontiguousarray(v) for k, v in arrays.items()}
    nc = bacc.Bacc("TRN2", target_bir_lowering=False, num_devices=1)
    args = [nc.dram_tensor(f"in_{k}", v.shape, F32, kind="ExternalInput").ap() for k, v in arrays.items()]
    out = nc.dram_tensor("out_rows", (P, N), F32, kind="ExternalOutput").ap()
    gnn_kernel(nc, *args, out)
    r = run_bass_kernel_spmd(nc, [{f"in_{k}": v for k, v in arrays.items()}], core_ids=[0])
    got = r.results[0]["out_rows"]
    return np.ascontiguousarray(got.reshape(P, BLOCKS, P).transpose(1, 0, 2).reshape(N, P))
```
